# Optimizing a Trainium2 kernel written in Bass

```python
import numpy as np
import jax
import jax.numpy as jnp

def _softmax(x, axis=-1):
    return jax.nn.softmax(x, axis=axis)

def _gelu(x):
    return jax.nn.gelu(x, approximate=True)

def _silu(x):
    return jax.nn.silu(x)

def _sigmoid(x):
    return jax.nn.sigmoid(x)

def _layernorm(x, axis=-1, eps=1e-05):
    m = jnp.mean(x, axis=axis, keepdims=True)
    v = jnp.var(x, axis=axis, keepdims=True)
    return (x - m) / jnp.sqrt(v + eps)

def _scatter_add(tgt, idx, src, axis=0):
    return tgt.at[idx].add(src)

def _segment_sum(src, seg, n):
    return jax.ops.segment_sum(src, seg, n)
kernel_name = 'mk_xattn_ffn_d1_seqx_r4_dd2202'

def setup_inputs(seed: int=0):
    np.random.seed(seed)
    _w = jnp.asarray

    def _rec_inputs():
        import jax
        import jax.numpy as jnp
        _rk = jax.random.key(seed)
        x = -0.000125 + 0.9999 * jax.random.normal(jax.random.fold_in(_rk, 1), (16, 256, 256), jnp.float32)
        _lenS = 256 - jax.random.randint(jax.random.fold_in(_rk, 7), (16,), 0, max(1, 256 // 4) + 1, jnp.int32)
        _lenS2 = 256 - jax.random.randint(jax.random.fold_in(_rk, 8), (16,), 0, max(1, 256 // 4) + 1, jnp.int32)
        _ctx_1024P = jax.random.normal(jax.random.fold_in(_rk, 11), (16, 16, 256), jnp.float32)
        _ctx_1024c = jax.random.dirichlet(jax.random.fold_in(_rk, 511), 0.3 * jnp.ones((16,), jnp.float32), (16, 256))
        _ctx_1024t = jnp.einsum('bsk,bkd->bsd', _ctx_1024c, _ctx_1024P)
        _ctx_1024t = _ctx_1024t * jax.lax.rsqrt(jnp.mean(jnp.square(_ctx_1024t)) + 1e-12) * 0.953939
        ctx_1024 = -1.52775e-05 + 0.999936 * (_ctx_1024t + 0.3 * jax.random.normal(jax.random.fold_in(_rk, 611), (16, 256, 256), jnp.float32))
        return (x, ctx_1024)
    x, ctx_1024 = _rec_inputs()

    def _L0_xattn_setup():
        import jax, jax.numpy as jnp
        import numpy as np
        D_MODEL = 256
        HEAD_SIZE = 256
        CONTEXT_SIZE = 128
        key = jax.random.key(seed)
        kq, kk, kv, kwq, kwk, kwv = jax.random.split(key, 6)
        B, S = (64, 128)
        scale = 1.0 / np.sqrt(D_MODEL)
        return {'query': jax.random.normal(kq, (B, S, D_MODEL), dtype=jnp.float32), 'key': jax.random.normal(kk, (B, S, D_MODEL), dtype=jnp.float32), 'value': jax.random.normal(kv, (B, S, D_MODEL), dtype=jnp.float32), 'w_q': jax.random.normal(kwq, (D_MODEL, HEAD_SIZE), dtype=jnp.float32) * scale, 'w_k': jax.random.normal(kwk, (D_MODEL, HEAD_SIZE), dtype=jnp.float32) * scale, 'w_v': jax.random.normal(kwv, (D_MODEL, HEAD_SIZE), dtype=jnp.float32) * scale, 'mask': 1}
    _L0_xattn_all = _L0_xattn_setup()
    _L0_xattn_in = {k: v for k, v in _L0_xattn_all.items() if k in ('w_q', 'w_k', 'w_v')}
    del _L0_xattn_all

    def _L0_ffn_setup():
        import jax, jax.numpy as jnp
        import numpy as np
        B, T, D = (2, 256, 256)
        H, DK, K = (8, 128, 8)
        NKEYS = 64
        NEXP = NKEYS * NKEYS

        def _rmsnorm(x, w, eps=1e-06):
            inv = jax.lax.rsqrt(jnp.mean(x * x, axis=-1, keepdims=True) + eps)
            return x * inv * w
        key = jax.random.key(seed)
        ks = jax.random.split(key, 5)
        return {'x': jax.random.normal(ks[0], (B, T, D), jnp.float32), 'w_q': jax.random.normal(ks[1], (H * 2 * DK, D), jnp.float32) * 0.02, 'keys': jax.random.normal(ks[2], (H, NKEYS, 2, DK), jnp.float32) * 0.02, 'expert_down': jax.random.normal(ks[3], (NEXP, D), jnp.float32) * 0.02, 'expert_up': jax.random.normal(ks[4], (NEXP, D), jnp.float32) * 0.02, 'norm_w': jnp.ones((D,), jnp.float32)}
    _L0_ffn_all = _L0_ffn_setup()
    _L0_ffn_in = {k: v for k, v in _L0_ffn_all.items() if k in ('w_q', 'keys', 'expert_down', 'expert_up', 'norm_w')}
    del _L0_ffn_all
    return {'x': x, 'ctx_1024': ctx_1024, 'L0_xattn_w_q': _L0_xattn_in['w_q'], 'L0_xattn_w_k': _L0_xattn_in['w_k'], 'L0_xattn_w_v': _L0_xattn_in['w_v'], 'L0_ffn_w_q': _L0_ffn_in['w_q'], 'L0_ffn_keys': _L0_ffn_in['keys'], 'L0_ffn_expert_down': _L0_ffn_in['expert_down'], 'L0_ffn_expert_up': _L0_ffn_in['expert_up'], 'L0_ffn_norm_w': _L0_ffn_in['norm_w']}

def reference(x, ctx_1024, L0_xattn_w_q, L0_xattn_w_k, L0_xattn_w_v, L0_ffn_w_q, L0_ffn_keys, L0_ffn_expert_down, L0_ffn_expert_up, L0_ffn_norm_w):
    import jax
    import jax.numpy as jnp

    def _L0_xattn_ref(query, key, value, w_q, w_k, w_v, mask):
        import jax, jax.numpy as jnp
        import numpy as np
        D_MODEL = 256
        HEAD_SIZE = 256
        CONTEXT_SIZE = 128
        q = jnp.einsum('bsd,dh->bsh', query, w_q)
        k = jnp.einsum('bsd,dh->bsh', key, w_k)
        v = jnp.einsum('bsd,dh->bsh', value, w_v)
        scale = 1.0 / np.sqrt(query.shape[-1]).astype(np.float32)
        scores = jnp.einsum('bqh,bkh->bqk', q, k) * scale
        if mask:
            S = scores.shape[1]
            causal = jnp.tril(jnp.ones((S, S), dtype=bool))
            scores = jnp.where(causal, scores, -jnp.inf)
        attn = jax.nn.softmax(scores, axis=-1)
        out = jnp.einsum('bqk,bkh->bqh', attn, v)
        return out

    def _L0_ffn_ref(x, w_q, keys, expert_down, expert_up, norm_w):
        import jax, jax.numpy as jnp
        import numpy as np
        B, T, D = (2, 256, 256)
        H, DK, K = (8, 128, 8)
        NKEYS = 64
        NEXP = NKEYS * NKEYS

        def _rmsnorm(x, w, eps=1e-06):
            inv = jax.lax.rsqrt(jnp.mean(x * x, axis=-1, keepdims=True) + eps)
            return x * inv * w
        b, t, d = x.shape
        xn = _rmsnorm(x, norm_w)
        q = (xn @ w_q.T).reshape(b, t, H, 2, DK)
        sim1 = jnp.einsum('bthd,hkd->bthk', q[..., 0, :], keys[:, :, 0, :])
        sim2 = jnp.einsum('bthd,hkd->bthk', q[..., 1, :], keys[:, :, 1, :])
        s1, i1 = jax.lax.top_k(sim1, K)
        s2, i2 = jax.lax.top_k(sim2, K)
        all_idx = (i1[..., :, None] * NKEYS + i2[..., None, :]).reshape(b, t, H, K * K)
        all_sc = (s1[..., :, None] + s2[..., None, :]).reshape(b, t, H, K * K)
        fs, pk = jax.lax.top_k(all_sc, K)
        fi = jnp.take_along_axis(all_idx, pk, axis=-1)
        wd = expert_down[fi]
        wu = expert_up[fi]
        hidden = jax.nn.gelu(jnp.einsum('btd,bthkd->bthk', xn, wd), approximate=False)
        hidden = hidden * jax.nn.relu(fs)
        return jnp.einsum('bthk,bthkd->btd', hidden, wu)
    x = x + _L0_xattn_ref(_layernorm(x, axis=-1), ctx_1024, ctx_1024, L0_xattn_w_q, L0_xattn_w_k, L0_xattn_w_v, 1)
    x = x + _L0_ffn_ref(_layernorm(x, axis=-1), L0_ffn_w_q, L0_ffn_keys, L0_ffn_expert_down, L0_ffn_expert_up, L0_ffn_norm_w)
    return x

_drawn_inputs = setup_inputs


def setup_inputs(seed=0):
    import zlib

    import numpy as np

    out = dict(_drawn_inputs(seed))
    spreads = {'L0_ffn_norm_w': (1.0, 0.6)}
    factors = {'L0_ffn_w_q': 6.796,
     'L0_ffn_keys': 6.724,
     'L0_ffn_expert_down': 6.813,
     'L0_ffn_expert_up': 6.665}
    for name, (base, spread) in spreads.items():
        noise = np.random.default_rng([zlib.crc32(name.encode()), seed]).standard_normal(out[name].shape)
        drawn = base * np.exp(spread * noise) if base else spread * noise
        out[name] = jnp.asarray(drawn.astype(out[name].dtype))
    for name, factor in factors.items():
        out[name] = (out[name] * factor).astype(out[name].dtype)
    return out
```

```python
from contextlib import ExitStack

import concourse.bass as bass
from concourse import mybir


def cross_attention_and_expert_ffn(
    nc: bass.Bass,
    x: bass.AP,
    ctx: bass.AP,
    attn_wq: bass.AP,
    attn_wk: bass.AP,
    attn_wv: bass.AP,
    ffn_wq: bass.AP,
    ffn_keys: bass.AP,
    expert_down: bass.AP,
    expert_up: bass.AP,
    norm_w: bass.AP,
    out: bass.AP,
):
    F32, F16 = mybir.dt.float32, mybir.dt.float16
    U16, I32 = mybir.dt.uint16, mybir.dt.int32
    ALU = mybir.AluOpType
    ACT = mybir.ActivationFunctionType
    X = mybir.AxisListType.X

    P = 128
    NBATCH, NTOK, D = x.shape
    NT = NTOK // P
    ND = D // P
    NHEAD, NKEY, _, DK = ffn_keys.shape
    K = 8
    NPICK = NHEAD * K
    NEXP = NKEY * NKEY
    NE = NEXP // P
    NPAIR = NE // 2
    NSIM = 2 * NHEAD * NKEY
    BANK = 512
    GT = 16
    NG = P // GT
    SLOTS = NPAIR
    FILLS = 12
    NEG = -3.0e38
    assert NT == 2 and ND == 2 and NPICK * 2 == P and NKEY * 2 == P and SLOTS == 2 * NG

    Z_SCALE = 2.0**10
    FULL = 2.0**14
    PICK_SCALE = 2.0**13
    HEADROOM = 2.0**-11
    ONE_OVER = 2130706432.0
    EXPONENT = 0x7F800000

    C_FRONT, C_PICK, C_HOT, C_FINAL = 39, 142, 16, 4

    es = ExitStack()
    with es:

        def sb(name, shape, dt=F32):
            return es.enter_context(nc.sbuf_tensor(name, shape, dt))

        def sem(name):
            return es.enter_context(nc.semaphore(name))

        down_t = sb("down_t", [P, 2, ND, NEXP], F16)
        up = sb("up", [P, NE, 2, D], F16)
        keys_q = sb("keys_q", [P, ND, NSIM])
        wqk = sb("wqk", [P, ND, D])
        wv = sb("wv", [P, ND, D])
        gelu_scale = sb("gelu_scale", [P, NE])
        s_scale = sb("s_scale", [P, 1])
        out_scale = sb("out_scale", [P, 1])
        ident = sb("ident", [P, P])
        ident16 = sb("ident16", [P, P], F16)
        col = sb("col", [P, P, GT], F16)
        causal = sb("causal", [P, 3 * P], mybir.dt.bfloat16)
        s_all = sb("s_all", [P, 2, NE, NTOK])
        sims = sb("sims", [P, NT, NSIM])
        z16 = sb("z16", [P, 3, 2, ND, NTOK], F16)
        x1 = sb("x1", [P, 3, NT, D])
        x_in = sb("x_in", [P, NT, D])
        ctx_in = sb("ctx_in", [P, NT, D])
        normed = sb("normed", [P, NT, D])
        normed_t = sb("normed_t", [P, ND, NTOK])
        ctx_t = sb("ctx_t", [P, ND, NTOK])
        q_t = sb("q_t", [P, ND, NTOK])
        v = sb("v", [P, NT, D])
        probs = sb("probs", [P, 3 * P])
        probs_t = normed[:].rearrange("p t d -> p (t d)")[:, 0 : 3 * P]
        stats = sb("stats", [P, NT, 6])
        mean_var = sb("mean_var", [P, NT, 2])
        var = sb("var", [P, NT])
        rstd = sb("rstd", [P, NT])
        newton = sb("newton", [P, NT])
        neg_max = sb("neg_max", [P, NT])
        row_sum = sb("row_sum", [P, NT])
        inv_sum = sb("inv_sum", [P, NT])
        top = sb("top", [P, 2, NHEAD, K])
        top_at = sb("top_at", [P, 2, NHEAD, K], U16)
        top_at16 = sb("top_at16", [P, 2, NHEAD, K], F16)
        best = sb("best", [P, NHEAD, K])
        best_at = sb("best_at", [P, NHEAD * K], U16)
        rank = sb("rank", [P, 2, NPICK], U16)
        key_of = sb("key_of", [P, 2, NPICK])
        key2 = sb("key2", [P, NPICK], U16)
        key2_low = sb("key2_low", [P, NPICK], U16)
        key2_high = sb("key2_high", [P, NPICK], U16)
        wmax = sb("wmax", [P, 1])
        wexp = sb("wexp", [P, 1])
        winv = sb("winv", [P, 1])
        weight = sb("weight", [P, NPICK])
        picks = sb("picks", [P, 4, NT, NPICK], F16)
        picks_t = sb("picks_t", [P, 4, P], F16)
        token_scale = sb("token_scale", [P, 3, NT])
        hot_a = sb("hot_a", [P, 2, P, GT], F16)
        hot_b = sb("hot_b", [P, 2, 2, NE, GT], F16)
        hot_j = sb("hot_j", [P, NE, GT], F16)
        work = hot_a[:, 0].rearrange("p c t -> p (c t)")
        sums = work[:, 0:1024].bitcast(F32).rearrange("p (h a) -> p h a", h=NHEAD)
        hit = work[:, 1024:2048].rearrange("p (s k a) -> p s k a", s=2, a=K)
        w32 = sb("w32", [P, 2, 2, NTOK])
        w_hi = sb("w_hi", [P, 2, 2, NTOK], F16)
        w_lo = sb("w_lo", [P, 2, 2, NTOK], F16)

        down_in, up_in = s_all[:, 0, :, :], s_all[:, 1, :, :]
        spare = up[:, :, :, :].rearrange("p a b c -> p (a b c)").bitcast(F32)
        ffn_wq_in = spare[:, 0:4096].rearrange("p (g d) -> p g d", d=D)
        keys_in = spare[:, 4096:5120].rearrange("p (s g c) -> p s g c", s=2, c=DK)
        keys_t = spare[:, 5120:6144].rearrange("p (s k) -> p s k", s=2)
        attn_in = spare[:, 6144:7168].rearrange("p (w a d) -> p w a d", w=2, a=ND)
        attn_t = spare[:, 7168:8192].rearrange("p (w a d) -> p w a d", w=2, a=ND)
        norm_col = sb("norm_col", [P, ND])
        norm_row = normed[:, 0, :]
        row_max = sb("row_max", [P, NE])
        up_max = sb("up_max", [P, 2])
        all_max = sb("all_max", [P, 2])
        row_scale = sb("row_scale", [P, NE])
        up_scale = sb("up_scale", [P, 1])
        up_exp = sb("up_exp", [P, 1])

        bank = [es.enter_context(nc.psum_tensor(f"bank{i}", [P, BANK], F32)) for i in range(8)]
        acc = bank[0:2]
        h_ps = bank[2:4]
        s_ps = bank[4:6]
        f_ps = bank[6:8]

        loaded = sem("loaded")
        weights_in = sem("weights_in")
        consts = sem("consts")
        setup_pe = sem("setup_pe")
        setup_act = sem("setup_act")
        setup_dve = sem("setup_dve")
        setup_pool = sem("setup_pool")
        settled = sem("settled")
        x_loaded = sem("x_loaded")
        ctx_loaded = sem("ctx_loaded")
        front_filled = sem("front_filled")
        normed_ready = sem("normed_ready")
        copied = sem("copied")
        scores_masked = sem("scores_masked")
        probs_ready = sem("probs_ready")
        x1_ready = sem("x1_ready")
        z_ready = sem("z_ready")
        z_lo_ready = sem("z_lo_ready")
        sims_used = sem("sims_used")
        dve_front = sem("dve_front")
        picks_ready = sem("picks_ready")
        picks_turned = sem("picks_turned")
        picks_t_ready = sem("picks_t_ready")
        hot_ready = sem("hot_ready")
        s_filled = sem("s_filled")
        s_stored = sem("s_stored")
        dve_pick = sem("dve_pick")
        dve_hot = sem("dve_hot")
        h_filled = sem("h_filled")
        gelu_ready = sem("gelu_ready")
        w_ready = sem("w_ready")
        w_hi_ready = sem("w_hi_ready")
        w_lo_ready = sem("w_lo_ready")
        up_done = sem("up_done")
        dve_final = sem("dve_final")
        out_ready = sem("out_ready")
        out_stored = sem("out_stored")

        COPIES = ["ctx_t", "normed_t", "v", "q_t", "probs_t", "z_t", "z_hi", "sim0", "sim1", "sim2", "sim3"]
        NCOPY = len(COPIES)

        def copy_no(b, name):
            return b * NCOPY + COPIES.index(name) + 1

        def after(eng, semaphore, count):
            if isinstance(count, int) and count <= 0:
                return
            eng.wait_ge(semaphore, count)

        def settle(eng):
            eng.sem_inc(settled, 1)

        class Steps:

            def __init__(self, eng, semaphore, start=0):
                self.eng, self.semaphore, self.start, self.n = eng, semaphore, start, 0

            def add(self, instruction):
                instruction.then_inc(self.semaphore, 1)
                self.n += 1

            def met(self):
                self.eng.wait_ge(self.semaphore, self.start + self.n)

            def link(self, instruction):
                self.add(instruction)
                self.met()

        STAGES = dict(front=(0, NBATCH), pick=(1, NBATCH + 1), dense=(2, NBATCH + 2), tail=(3, NBATCH + 3))

        def passes(eng, body):
            for it in range(0, 3):
                body(it, {s for s, (a, z) in STAGES.items() if a <= it < z})
            with eng.Fori(3, NBATCH) as it:
                body(it, set(STAGES))
            for it in range(NBATCH, NBATCH + 3):
                body(it, {s for s, (a, z) in STAGES.items() if a <= it < z})

        def lagged(stages, k, lag):
            return "dense" in stages if k >= lag else "tail" in stages

        block = es.enter_context(nc.Block())

        @block.sync
        def _(sp):
            for a in range(2):
                for w, src in ((down_in, expert_down), (up_in, expert_up)):
                    v4 = src.rearrange("(i j2 jp) d -> jp i j2 d", j2=NE, jp=2)
                    sp.dma_start(w[a * NKEY : (a + 1) * NKEY], v4[a]).then_inc(weights_in, 16)
            sp.dma_start(norm_row, norm_w.partition_broadcast(P)).then_inc(weights_in, 16)

            def load_x(b):
                after(sp, x1_ready, b)
                sp.dma_start(x_in[:], x[b].rearrange("(t p) d -> p t d", p=P)).then_inc(x_loaded, 16)

            def load_ctx(b):
                after(sp, front_filled, (b - 1) * FILLS + 1 if not isinstance(b, int) or b > 0 else 0)
                sp.dma_start(ctx_in[:], ctx[b].rearrange("(t p) d -> p t d", p=P)).then_inc(ctx_loaded, 16)

            load_x(0)
            load_ctx(0)

            def body(it, stages):
                if "tail" in stages:
                    sp.wait_ge(out_ready, it - 2)
                    sp.dma_start(
                        out[it - 3].rearrange("(t p) d -> p t d", p=P), x1[:, it % 3, :, :]
                    ).then_inc(out_stored, 16)
                if "front" in stages and not (isinstance(it, int) and it == NBATCH - 1):
                    load_ctx(it + 1)
                    load_x(it + 1)

            for it in range(0, 3):
                body(it, {"front"})
            with sp.Fori(3, NBATCH - 1) as it:
                body(it, {"front", "tail"})
            for it in range(NBATCH - 1, NBATCH + 3):
                body(it, {"tail"})
            sp.wait_ge(out_stored, 16 * NBATCH)

        @block.gpsimd
        def _(pool):
            st = Steps(pool, setup_pool)
            pool.dma_start(ffn_wq_in, ffn_wq.rearrange("(g p) d -> p g d", p=P)).then_inc(loaded, 16)
            kv = ffn_keys.rearrange("(g h) k s c -> (h k) s g c", h=2)
            for s in range(2):
                pool.dma_start(keys_in[:, s], kv[:, s]).then_inc(loaded, 16)
            for w, src in ((attn_in[:, 0], attn_wq), (attn_in[:, 1], attn_wk), (wv[:], attn_wv)):
                pool.dma_start(w, src.rearrange("(a p) n -> p a n", p=P)).then_inc(loaded, 16)
            pool.dma_start(norm_col[:], norm_w.rearrange("(a p) -> p a", p=P),
                           allow_slow_non_contiguous=True).then_inc(loaded, 16)
            st.add(nc.gpsimd.memset(ident[:], 0.0))
            st.add(nc.gpsimd.memset(ident16[:], 0.0))
            st.add(nc.gpsimd.memset(causal[:], 0.0))
            st.add(nc.gpsimd.iota(col[:], [[1, P], [0, GT]], base=0, channel_multiplier=0,
                                  allow_small_or_imprecise_dtypes=True))
            st.met()
            for m in (ident, ident16):
                st.add(nc.gpsimd.affine_select(out=m[:], in_=m[:], compare_op=ALU.not_equal, fill=1.0, base=0,
                                               pattern=[[-1, P]], channel_multiplier=1))
            for c in (0, 2 * P):
                st.add(nc.gpsimd.affine_select(out=causal[:, c : c + P], in_=causal[:, c : c + P],
                                               compare_op=ALU.is_ge, fill=NEG, base=0,
                                               pattern=[[-1, P]], channel_multiplier=1))
            st.met()
            nc.gpsimd.memset(newton[:], 0.0).then_inc(consts, 1)
            pool.wait_ge(setup_dve, MAX_READY)
            nc.gpsimd.partition_all_reduce(all_max[:], up_max[:], P, bass.bass_isa.ReduceOp.max).then_inc(setup_pool, 1)

            def body(it, stages):
                if "dense" not in stages:
                    return
                b = it - 2
                for k in range(SLOTS):
                    pool.wait_ge(gelu_ready, b * NPAIR + k + 1)
                    if k == 0:
                        pool.wait_ge(s_stored, (b + 1) * NG)
                    nc.gpsimd.tensor_tensor(w32[:, k % 2], w32[:, k % 2], s_all[:, it % 2, 2 * k : 2 * k + 2, :],
                                            ALU.mult).then_inc(w_ready, 1)

            passes(pool, body)

        @block.scalar
        def _(act):
            st = Steps(act, setup_act)
            act.wait_ge(setup_pe, 1)
            st.add(nc.scalar.activation(attn_t[:, 0].rearrange("p a d -> p (a d)"), bank[0][:], ACT.Copy))
            st.add(nc.scalar.activation(attn_t[:, 1].rearrange("p a d -> p (a d)"), bank[1][:], ACT.Copy))
            act.wait_ge(setup_pe, 2)
            st.add(nc.scalar.activation(wqk[:].rearrange("p a d -> p (a d)"), bank[2][:], ACT.Copy, scale=float(D) ** -0.5))
            act.wait_ge(setup_pe, 3)
            for s in range(2):
                st.add(nc.scalar.activation(keys_t[:, s], bank[4 + s][:], ACT.Copy))
            for g in range(NE * ND // 4):
                act.wait_ge(setup_pe, 5 + g)
                a, q = g % ND, g // ND
                st.add(nc.scalar.activation(down_t[:, 0, a, q * BANK : (q + 1) * BANK], bank[g % 4][:], ACT.Copy))

            def copy(dst, src, **kw):
                nc.scalar.activation(dst, src, ACT.Copy, **kw).then_inc(copied, 1)

            def flat(t):
                return t.rearrange("p a d -> p (a d)")

            def body(it, stages):
                for k in range(SLOTS):
                    n = (it - 2) * NPAIR + k
                    if "dense" in stages:
                        act.wait_ge(h_filled, n + 1)
                        after(act, w_lo_ready, n - 1)
                        after(act, w_hi_ready, n - 1)
                        for e in range(2):
                            g = nc.scalar.activation(w32[:, k % 2, e, :], h_ps[k % 2][:, e * NTOK : (e + 1) * NTOK],
                                                     ACT.Gelu, scale=gelu_scale[:, 2 * k + e : 2 * k + e + 1])
                        g.then_inc(gelu_ready, 1)
                    if lagged(stages, k, 1):
                        act.wait_ge(w_ready, n)
                        after(act, up_done, n - 2)
                        nc.scalar.activation(w_hi[:, (k - 1) % 2], w32[:, (k - 1) % 2], ACT.Copy).then_inc(w_hi_ready, 1)
                    if "front" in stages:
                        b = it

                        def filled(i):
                            act.wait_ge(front_filled, b * FILLS + i + 1)

                        if k == 0:
                            filled(0)
                            copy(flat(ctx_t[:]), f_ps[0][:])
                        if k == 1:
                            filled(1)
                            copy(flat(normed_t[:]), f_ps[1][:])
                            filled(2)
                            copy(flat(v[:]), f_ps[0][:])
                        if k == 2:
                            filled(3)
                            copy(flat(q_t[:]), f_ps[1][:])
                        if k == 3:
                            act.wait_ge(scores_masked, b + 1)
                            e0 = nc.scalar.activation(probs[:, 0:P], probs[:, 0:P], ACT.Exp,
                                                      bias=neg_max[:, 0:1], accum_out=row_sum[:, 0:1])
                            e0.then_inc(probs_ready, 1)
                            e1 = nc.scalar.activation(probs[:, P : 3 * P], probs[:, P : 3 * P], ACT.Exp,
                                                      bias=neg_max[:, 1:2], accum_out=row_sum[:, 1:2])
                            e1.then_inc(probs_ready, 1)
                        if k == 4:
                            filled(5)
                            copy(probs_t, f_ps[1][:, 0 : 3 * P])
                        if k == 7:
                            filled(7)
                            copy(flat(normed_t[:]), f_ps[1][:])
                            after(act, h_filled, (it - 2) * NPAIR)
                            copy(z16[:, it % 3, 0].rearrange("p a d -> p (a d)"), f_ps[1][:])
                        if 9 <= k < 13:
                            i = k - 9
                            filled(8 + i)
                            after(act, sims_used, (b - 1) * NT + i // 2 + 1 if not isinstance(b, int) or b > 0 else 0)
                            copy(sims[:, i // 2, (i % 2) * BANK : (i % 2 + 1) * BANK], f_ps[i % 2][:])
                    if "pick" in stages:
                        b = it - 1
                        if k == NG - 1:
                            act.wait_ge(picks_turned, b + 1)
                            after(act, hot_ready, b * NG)
                            nc.scalar.activation(picks_t[:].rearrange("p q t -> p (q t)"),
                                                 s_ps[0][:].bitcast(F16)[:, 0 : 4 * P], ACT.Copy).then_inc(picks_t_ready, 1)
                        if k >= NG:
                            g = k - NG
                            if g == 0:
                                after(act, w_ready, (b - 1) * NPAIR)
                            act.wait_ge(s_filled, b * NG + g + 1)
                            for t in range(NT):
                                s = nc.scalar.activation(
                                    s_all[:, (it + 1) % 2, :, t * P + g * GT : t * P + (g + 1) * GT],
                                    s_ps[t][:].rearrange("p (j t) -> p j t", t=GT), ACT.Copy, scale=s_scale[:, 0:1])
                            s.then_inc(s_stored, 1)

            passes(act, body)

        @block.vector
        def _(dve):
            st = Steps(dve, setup_dve)

            def ts(o, i, s1, s2, op0, op1=None):
                return nc.vector.tensor_scalar(o, i, s1, s2, op0, op1) if op1 is not None else nc.vector.tensor_scalar(
                    o, i, s1, s2, op0)

            def power_of_two(o, i, steps):
                steps.link(ts(o.bitcast(I32), i.bitcast(I32), EXPONENT, None, ALU.bitwise_and))

            def inverse(o, i, steps):
                steps.link(ts(o.bitcast(I32), i.bitcast(I32), -1.0, ONE_OVER, ALU.mult, ALU.add))

            dve.wait_ge(weights_in, 16 * 5)
            st.link(nc.vector.tensor_tensor(down_in, down_in, norm_row.unsqueeze(1).to_broadcast([P, NE, D]), ALU.mult))
            st.add(nc.vector.tensor_reduce(row_max[:], down_in, X, ALU.max, apply_absolute_value=True))
            st.link(nc.vector.tensor_reduce(up_max[:, 1:2], up_in.rearrange("p a b -> p (a b)"), X, ALU.max,
                                            apply_absolute_value=True))
            st.link(nc.vector.tensor_reduce(up_max[:, 0:1], row_max[:], X, ALU.max))
            assert st.n == MAX_READY
            st.link(ts(row_max[:], row_max[:], 1e-30, None, ALU.max))
            power_of_two(row_scale[:], row_max[:], st)
            st.add(ts(gelu_scale[:], row_scale[:], 1.0 / (FULL * Z_SCALE), None, ALU.mult))
            inverse(row_max[:], row_scale[:], st)
            for j in range(NE):
                st.add(ts(down_in[:, j, :], down_in[:, j, :], row_max[:, j : j + 1], FULL, ALU.mult, ALU.mult))
            assert st.n == DOWN_READY, st.n
            for a in range(ND):
                for s in range(2):
                    dve.wait_ge(setup_pe, 4)
                    st.add(ts(keys_q[:, a, s * BANK : (s + 1) * BANK], bank[4 + 2 * a + s][:], norm_col[:, a : a + 1],
                              1.0 / Z_SCALE, ALU.mult, ALU.mult))
            dve.wait_ge(setup_pool, 9)
            st.link(ts(all_max[:], all_max[:], 1e-30, None, ALU.max))
            power_of_two(all_max[:], all_max[:], st)
            st.add(ts(up_exp[:], all_max[:, 1:2], 1.0 / FULL, None, ALU.mult))
            inverse(s_scale[:], all_max[:, 0:1], st)
            inverse(up_scale[:], all_max[:, 1:2], st)
            st.link(ts(s_scale[:], s_scale[:], HEADROOM, None, ALU.mult))
            st.link(ts(out_scale[:], all_max[:, 0:1], up_exp[:], 1.0 / (PICK_SCALE * HEADROOM), ALU.mult, ALU.mult))
            st.link(ts(up_in.rearrange("p a b -> p (a b)"), up_in.rearrange("p a b -> p (a b)"), up_scale[:], FULL,
                       ALU.mult, ALU.mult))
            dve.wait_ge(setup_pe, 4)
            st.link(nc.vector.tensor_copy(up[:, :, 0, :], up_in))
            st.link(nc.vector.tensor_tensor(up[:, :, 1, :], up_in, up[:, :, 0, :], ALU.subtract))
            assert st.n == LO_START, st.n
            for g in range(NE * ND // 4):
                dve.wait_ge(setup_act, 5 + g + 1)
                a, q = g % ND, g // ND
                cols = slice(q * BANK, (q + 1) * BANK)
                st.add(nc.vector.tensor_tensor(down_t[:, 1, a, cols], bank[g % 4][:], down_t[:, 0, a, cols], ALU.subtract))
            st.met()

            def normalise(src, steps, factor, eps, scale, ready):
                for t in range(NT):
                    steps.add(nc.vector.bn_stats(stats[:, t, :], src(t)))
                steps.met()
                settle(dve)
                for t in range(NT):
                    steps.add(nc.vector.bn_aggr(mean_var[:, t, :], stats[:, t, :]))
                steps.met()
                steps.link(ts(var[:], mean_var[:, :, 1], factor, eps, ALU.mult, ALU.add))
                steps.link(ts(rstd[:].bitcast(I32), var[:].bitcast(I32), 1, None, ALU.logical_shift_right))
                steps.link(ts(rstd[:].bitcast(I32), rstd[:].bitcast(I32), -1.0, float(0x5F3759DF), ALU.mult, ALU.add))
                for _ in range(3):
                    steps.link(nc.vector.tensor_tensor(newton[:], rstd[:], rstd[:], ALU.mult))
                    steps.link(nc.vector.scalar_tensor_tensor(newton[:], newton[:], -0.5, var[:], ALU.mult, ALU.mult))
                    steps.link(nc.vector.scalar_tensor_tensor(rstd[:], newton[:], 1.5, rstd[:], ALU.add, ALU.mult))
                if scale != 1.0:
                    steps.link(ts(rstd[:], rstd[:], scale, None, ALU.mult))
                for t in range(NT):
                    last = ts(normed[:, t, :], src(t), mean_var[:, t, 0:1], rstd[:, t : t + 1], ALU.subtract, ALU.mult)
                    last.then_inc(ready, 1)

            def body(it, stages):
                front = Steps(dve, dve_front, it * C_FRONT)
                pick = Steps(dve, dve_pick, (it - 1) * C_PICK)
                hot = Steps(dve, dve_hot, (it - 1) * C_HOT)
                fin = Steps(dve, dve_final, (it - 3) * C_FINAL)
                for k in range(SLOTS):
                    n = (it - 2) * NPAIR + k
                    if lagged(stages, k, 1):
                        dve.wait_ge(w_hi_ready, n)
                        after(dve, up_done, n - 2)
                        nc.vector.tensor_tensor(w_lo[:, (k - 1) % 2], w32[:, (k - 1) % 2], w_hi[:, (k - 1) % 2],
                                                ALU.subtract).then_inc(w_lo_ready, 1)
                    if "tail" in stages and k == 2:
                        dve.wait_ge(up_done, (it - 2) * NPAIR)
                        for half in range(2):
                            for t in range(NT):
                                o = x1[:, it % 3, t, :]
                                s = nc.vector.scalar_tensor_tensor(
                                    o, acc[t][:, half * D : (half + 1) * D], token_scale[:, it % 3, t : t + 1], o,
                                    ALU.mult, ALU.add)
                                fin.add(s)
                            fin.met()
                        dve.sem_inc(out_ready, 1)
                    if "front" in stages:
                        b = it
                        if k == 0:
                            dve.wait_ge(x_loaded, 16 * (b + 1))
                            after(dve, front_filled, (b - 1) * FILLS + 8 if not isinstance(b, int) or b > 0 else 0)
                            normalise(lambda t: x_in[:, t, :], front, 1.0, 1e-5, 1.0, normed_ready)
                        if k == 3:
                            dve.wait_ge(front_filled, b * FILLS + 5)
                            after(dve, front_filled, (b - 1) * FILLS + 6 if not isinstance(b, int) or b > 0 else 0)
                            front.link(nc.vector.tensor_tensor(probs[:], f_ps[0][:, 0 : 3 * P], causal[:], ALU.add))
                            front.add(nc.vector.tensor_reduce(neg_max[:, 0:1], probs[:, 0:P], X, ALU.max, negate=True))
                            front.link(nc.vector.tensor_reduce(neg_max[:, 1:2], probs[:, P : 3 * P], X, ALU.max, negate=True))
                            dve.sem_inc(scores_masked, 1)
                        if k == 5:
                            dve.wait_ge(probs_ready, 2 * (b + 1))
                            front.link(nc.vector.reciprocal(inv_sum[:], row_sum[:]))
                            dve.wait_ge(front_filled, b * FILLS + 7)
                            after(dve, out_stored, (it - 2) * 16)
                            for t in range(NT):
                                front.add(nc.vector.scalar_tensor_tensor(
                                    x1[:, it % 3, t, :], f_ps[0][:, t * D : (t + 1) * D], inv_sum[:, t : t + 1],
                                    x_in[:, t, :], ALU.mult, ALU.add))
                            front.met()
                            dve.sem_inc(x1_ready, 1)
                            normalise(lambda t: x1[:, it % 3, t, :], front, 1.0 + 1e-6, 1e-11, Z_SCALE, z_ready)
                        if k == 7:
                            dve.wait_ge(copied, copy_no(b, "z_hi"))
                            after(dve, h_filled, (it - 2) * NPAIR)
                            nc.vector.tensor_tensor(
                                z16[:, it % 3, 1].rearrange("p a d -> p (a d)"), f_ps[1][:],
                                z16[:, it % 3, 0].rearrange("p a d -> p (a d)"), ALU.subtract).then_inc(z_lo_ready, 1)
                    if "pick" in stages:
                        b = it - 1
                        t, part = divmod(k, 3)
                        if k < 6 and part == 0:
                            dve.wait_ge(copied, copy_no(b, "sim1" if t == 0 else "sim3"))
                            settle(dve)
                            for s in range(2):
                                for h in range(NHEAD):
                                    c = (s * NHEAD + h) * NKEY
                                    pick.add(nc.vector.max(top[:, s, h, :], sims[:, t, c : c + NKEY]))
                            pick.met()
                            settle(dve)
                            for s in range(2):
                                for h in range(NHEAD):
                                    c = (s * NHEAD + h) * NKEY
                                    pick.add(nc.vector.max_index(top_at[:, s, h, :], top[:, s, h, :], sims[:, t, c : c + NKEY]))
                            pick.met()
                            dve.sem_inc(sims_used, 1)
                        if k < 6 and part == 1:
                            if t == 0:
                                after(dve, s_filled, b * NG)
                            pick.add(nc.vector.tensor_copy(top_at16[:], top_at[:]))
                            pick.link(nc.vector.tensor_tensor(
                                sums.rearrange("p h (a b) -> p h a b", a=K),
                                top[:, 0].unsqueeze(3).to_broadcast([P, NHEAD, K, K]),
                                top[:, 1].unsqueeze(2).to_broadcast([P, NHEAD, K, K]), ALU.add))
                            settle(dve)
                            for h in range(NHEAD):
                                pick.add(nc.vector.max(best[:, h, :], sums[:, h, :]))
                            pick.met()
                            settle(dve)
                            for h in range(NHEAD):
                                pick.add(nc.vector.max_index(best_at[:, h * K : (h + 1) * K], best[:, h, :], sums[:, h, :]))
                            pick.met()
                        if k < 6 and part == 2:
                            pick.add(ts(rank[:, 0], best_at[:], 3, None, ALU.logical_shift_right))
                            pick.link(ts(rank[:, 1], best_at[:], K - 1, None, ALU.bitwise_and))
                            for s in range(2):
                                pick.add(nc.vector.tensor_tensor(
                                    hit[:, s], rank[:, s].unsqueeze(2).to_broadcast([P, NPICK, K]),
                                    col[:, 0:K, 0].unsqueeze(1).to_broadcast([P, NPICK, K]), ALU.is_equal))
                            pick.met()
                            for s in range(2):
                                h4 = hit[:, s].rearrange("p (h k) a -> p h k a", k=K)
                                pick.add(nc.vector.tensor_tensor(
                                    h4, h4, top_at16[:, s].unsqueeze(2).to_broadcast([P, NHEAD, K, K]), ALU.mult))
                            pick.met()
                            pick.link(nc.vector.tensor_reduce(key_of[:], hit, X, ALU.add))
                            pick.link(nc.vector.tensor_copy(key2[:], key_of[:, 1]))
                            pick.add(ts(key2_low[:], key2[:], 1, None, ALU.bitwise_and))
                            pick.add(ts(key2_high[:], key2[:], 1, None, ALU.logical_shift_right))
                            pick.met()
                            if t == 0:
                                after(dve, picks_turned, b)
                            pick.add(nc.vector.scalar_tensor_tensor(picks[:, 0, t, :], key2_low[:], float(NKEY),
                                                                    key_of[:, 0], ALU.mult, ALU.add))
                            pick.add(nc.vector.tensor_copy(picks[:, 1, t, :], key2_high[:]))
                            pick.link(nc.vector.tensor_reduce(wmax[:], best[:, :, 0], X, ALU.max))
                            pick.link(ts(wmax[:], wmax[:], 1e-30, 1e30, ALU.max, ALU.min))
                            power_of_two(wexp[:], wmax[:], pick)
                            inverse(winv[:], wexp[:], pick)
                            pick.link(ts(winv[:], winv[:], PICK_SCALE, None, ALU.mult))
                            pick.add(ts(token_scale[:, (it + 2) % 3, t : t + 1], wexp[:], out_scale[:], None, ALU.mult))
                            pick.link(ts(weight[:], best[:].rearrange("p h k -> p (h k)"), 0.0, winv[:], ALU.max, ALU.mult))
                            pick.link(nc.vector.tensor_copy(picks[:, 2, t, :], weight[:]))
                            pick.link(nc.vector.tensor_tensor(picks[:, 3, t, :], weight[:], picks[:, 2, t, :], ALU.subtract))
                            dve.sem_inc(picks_ready, 1)
                        if k >= NG - 1 and k < 2 * NG - 1:
                            g = k - (NG - 1)
                            if g == 0:
                                dve.wait_ge(picks_t_ready, b + 1)
                            after(dve, s_filled, b * NG + g - 1)
                            cols = slice(g * GT, (g + 1) * GT)
                            hot.add(nc.vector.tensor_tensor(
                                hot_a[:, g % 2], picks_t[:, 0, cols].unsqueeze(1).to_broadcast([P, P, GT]),
                                col[:], ALU.is_equal))
                            after(dve, hot_ready, b * NG + g)
                            hot.add(nc.vector.tensor_tensor(
                                hot_j[:], picks_t[:, 1, cols].unsqueeze(1).to_broadcast([P, NE, GT]),
                                col[:, 0:NE, :], ALU.is_equal))
                            hot.met()
                            nc.vector.tensor_tensor(
                                hot_b[:, g % 2], hot_j[:].unsqueeze(1).to_broadcast([P, 2, NE, GT]),
                                picks_t[:, 2:4, cols].unsqueeze(2).to_broadcast([P, 2, NE, GT]),
                                ALU.mult).then_inc(hot_ready, 1)
                for name, steps, count, stage in (("front", front, C_FRONT, "front"), ("pick", pick, C_PICK, "pick"),
                                                  ("hot", hot, C_HOT, "pick"), ("final", fin, C_FINAL, "tail")):
                    assert steps.n == (count if stage in stages else 0), (name, steps.n)

            passes(dve, body)

        @block.tensor
        def _(pe):
            mm, turn = nc.tensor.matmul, nc.tensor.transpose
            pe.wait_ge(loaded, 16 * 7)
            pe.wait_ge(consts, 1)
            for w in range(2):
                for a in range(ND):
                    for c in range(ND):
                        t = turn(bank[w][:, c * D + a * P : c * D + (a + 1) * P], attn_in[:, w, a, c * P : (c + 1) * P],
                                 ident[:])
            t.then_inc(setup_pe, 1)
            pe.wait_ge(setup_act, 2)
            for a in range(ND):
                for c in range(ND):
                    t = mm(bank[2][:, a * D : (a + 1) * D], attn_t[:, 0, c, a * P : (a + 1) * P], attn_t[:, 1, c, :],
                           start=(c == 0), stop=(c == ND - 1))
            t.then_inc(setup_pe, 1)
            for s in range(2):
                for g in range(NHEAD // 2):
                    t = turn(bank[4 + s][:, g * P : (g + 1) * P], keys_in[:, s, g, :], ident[:])
            t.then_inc(setup_pe, 1)
            pe.wait_ge(setup_act, 5)
            for a in range(ND):
                for s in range(2):
                    for h in range(NHEAD):
                        t = mm(bank[4 + 2 * a + s][:, h * NKEY : (h + 1) * NKEY],
                               ffn_wq_in[:, 2 * h + s, a * P : (a + 1) * P], keys_t[:, s, h * NKEY : (h + 1) * NKEY],
                               start=True, stop=True)
            t.then_inc(setup_pe, 1)
            pe.wait_ge(setup_dve, DOWN_READY)
            for g in range(NE * ND // 4):
                a, q = g % ND, g // ND
                after(pe, setup_dve, LO_START + g - 4 + 1 if g >= 4 else 0)
                for i in range(4):
                    t = turn(bank[g % 4][:, i * P : (i + 1) * P], down_in[:, 4 * q + i, a * P : (a + 1) * P], ident[:])
                t.then_inc(setup_pe, 1)
            pe.wait_ge(setup_dve, LO_START + NE * ND // 4)

            def body(it, stages):
                for k in range(SLOTS):
                    n = (it - 2) * NPAIR + k
                    if "dense" in stages:
                        if k == 0:
                            pe.wait_ge(z_lo_ready, it - 1)
                        after(pe, gelu_ready, n - 1)
                        for e in range(2):
                            j = 2 * k + e
                            terms = [(gp, zp, a) for gp, a in ((0, 0), (0, 1), (1, 0), (1, 1)) for zp in range(2 - gp)]
                            for i, (gp, zp, a) in enumerate(terms):
                                h = mm(h_ps[k % 2][:, e * NTOK : (e + 1) * NTOK], down_t[:, gp, a, j * P : (j + 1) * P],
                                       z16[:, (it + 1) % 3, zp, a, :], start=(i == 0), stop=(i == len(terms) - 1))
                        h.then_inc(h_filled, 1)
                    if "front" in stages:
                        front(it, k)
                    if "pick" in stages:
                        b = it - 1
                        if k == NG - 1:
                            pe.wait_ge(picks_ready, NT * (b + 1))
                            after(pe, s_stored, b * NG)
                            turned = s_ps[0][:].bitcast(F16)
                            for q in range(4):
                                t = turn(turned[:, q * P : (q + 1) * P], picks[:, q].rearrange("p t k -> p (t k)"),
                                         ident16[:])
                            t.then_inc(picks_turned, 1)
                        if k >= NG:
                            g = k - NG
                            pe.wait_ge(hot_ready, b * NG + g + 1)
                            if g == 0:
                                pe.wait_ge(picks_t_ready, b + 1)
                            else:
                                pe.wait_ge(s_stored, b * NG + g)
                            for i in range(GT):
                                for part in range(2):
                                    for t in range(NT):
                                        rows = slice(t * NPICK, (t + 1) * NPICK)
                                        o = s_ps[t][:].rearrange("p (j t) -> p j t", t=GT)
                                        m = mm(o[:, :, i], hot_a[rows, g % 2, :, i], hot_b[rows, g % 2, part, :, i],
                                               start=(part == 0), stop=(part == 1))
                            m.then_inc(s_filled, 1)
                    if lagged(stages, k, 2):
                        j = (k - 2) % NPAIR
                        pe.wait_ge(w_hi_ready, n - 1)
                        pe.wait_ge(w_lo_ready, n - 1)
                        if j == 0:
                            after(pe, out_ready, it - 2)
                        for t in range(NT):
                            for e in range(2):
                                cols = slice(t * P, (t + 1) * P)
                                mm(acc[t][:, 0 : 2 * D], w_hi[:, j % 2, e, cols],
                                   up[:, 2 * j + e].rearrange("p q d -> p (q d)"),
                                   start=(j == 0 and e == 0), stop=False)
                                u = mm(acc[t][:, 0:D], w_lo[:, j % 2, e, cols], up[:, 2 * j + e, 0, :],
                                       start=False, stop=(j == NPAIR - 1 and e == 1))
                        u.then_inc(up_done, 1)

            def front(b, k):
                def fill(m):
                    m.then_inc(front_filled, 1)

                def turn_tiles(dst, src):
                    for a in range(ND):
                        for t in range(NT):
                            m = turn(dst[:, a * NTOK + t * P : a * NTOK + (t + 1) * P], src[:, t, a * P : (a + 1) * P],
                                     ident[:])
                    fill(m)

                def from_(name):
                    pe.wait_ge(copied, copy_no(b, name))

                if k == 0:
                    pe.wait_ge(ctx_loaded, 16 * (b + 1))
                    after(pe, copied, copy_no(b - 1, "sim2") if not isinstance(b, int) or b > 0 else 0)
                    turn_tiles(f_ps[0], ctx_in)
                if k == 1:
                    pe.wait_ge(normed_ready, NT * (b + 1))
                    after(pe, copied, copy_no(b - 1, "sim3") if not isinstance(b, int) or b > 0 else 0)
                    turn_tiles(f_ps[1], normed)
                    from_("ctx_t")
                    for t in range(NT):
                        for a in range(ND):
                            m = mm(f_ps[0][:, t * D : (t + 1) * D], ctx_t[:, a, t * P : (t + 1) * P], wv[:, a, :],
                                   start=(a == 0), stop=(a == ND - 1))
                    fill(m)
                if k == 2:
                    from_("normed_t")
                    for c in range(ND):
                        for a in range(ND):
                            m = mm(f_ps[1][:, c * NTOK : (c + 1) * NTOK], wqk[:, a, c * P : (c + 1) * P],
                                   normed_t[:, a, :], start=(a == 0), stop=(a == ND - 1))
                    fill(m)
                if k == 3:
                    from_("q_t")
                    for t in range(NT):
                        for a in range(ND):
                            m = mm(f_ps[0][:, t * P : (2 * t + 1) * P], q_t[:, a, t * P : (t + 1) * P],
                                   ctx_t[:, a, 0 : (t + 1) * P], start=(a == 0), stop=(a == ND - 1))
                    fill(m)
                if k == 4:
                    pe.wait_ge(probs_ready, 2 * (b + 1))
                    for i in range(3):
                        m = turn(f_ps[1][:, i * P : (i + 1) * P], probs[:, i * P : (i + 1) * P], ident[:])
                    fill(m)
                if k == 5:
                    from_("probs_t")
                    for t, blocks in ((0, (0,)), (1, (1, 2))):
                        for i, c in enumerate(blocks):
                            m = mm(f_ps[0][:, t * D : (t + 1) * D], probs_t[:, c * P : (c + 1) * P], v[:, i, :],
                                   start=(i == 0), stop=(i == len(blocks) - 1))
                    fill(m)
                if k == 7:
                    pe.wait_ge(z_ready, NT * (b + 1))
                    turn_tiles(f_ps[1], normed)
                if 9 <= k < 13:
                    i = k - 9
                    t, c = i // 2, i % 2
                    if i == 0:
                        from_("z_hi")
                    if i == 1:
                        pe.wait_ge(z_lo_ready, b + 1)
                    if i >= 2:
                        from_(f"sim{i - 2}")
                    for a in range(ND):
                        m = mm(f_ps[c][:, :], normed_t[:, a, t * P : (t + 1) * P],
                               keys_q[:, a, c * BANK : (c + 1) * BANK], start=(a == 0), stop=(a == ND - 1))
                    fill(m)

            passes(pe, body)


MAX_READY = 4
DOWN_READY = 40
LO_START = 54


_INS = ["x", "ctx_1024", "L0_xattn_w_q", "L0_xattn_w_k", "L0_xattn_w_v", "L0_ffn_w_q", "L0_ffn_keys",
        "L0_ffn_expert_down", "L0_ffn_expert_up", "L0_ffn_norm_w"]


def kernel(**inputs):
    import numpy as np
    import concourse.bacc as bacc
    from concourse.bass_utils import run_bass_kernel_spmd

    nc = bacc.Bacc("TRN2", target_bir_lowering=False, num_devices=1)
    arrays, args = {}, []
    for name in _INS:
        a = np.ascontiguousarray(inputs[name])
        arrays[f"in_{name}"] = a
        args.append(nc.dram_tensor(f"in_{name}", a.shape, mybir.dt.from_np(a.dtype), kind="ExternalInput").ap())
    shape = arrays["in_x"].shape
    args.append(nc.dram_tensor("out_dram", shape, mybir.dt.float32, kind="ExternalOutput").ap())
    cross_attention_and_expert_ffn(nc, *args)
    return run_bass_kernel_spmd(nc, [arrays], core_ids=[0]).results[0]["out_dram"]
```

```python
from contextlib import ExitStack

import concourse.bass as bass
from concourse import mybir


def cross_attention_and_expert_ffn(
    nc: bass.Bass,
    x: bass.AP,
    ctx: bass.AP,
    attn_wq: bass.AP,
    attn_wk: bass.AP,
    attn_wv: bass.AP,
    ffn_wq: bass.AP,
    ffn_keys: bass.AP,
    expert_down: bass.AP,
    expert_up: bass.AP,
    norm_w: bass.AP,
    out: bass.AP,
):
    F32, F16 = mybir.dt.float32, mybir.dt.float16
    U16, I32 = mybir.dt.uint16, mybir.dt.int32
    ALU = mybir.AluOpType
    ACT = mybir.ActivationFunctionType
    X = mybir.AxisListType.X

    P = 128
    NBATCH, NTOK, D = x.shape
    NT = NTOK // P
    ND = D // P
    NHEAD, NKEY, _, DK = ffn_keys.shape
    K = 8
    NPICK = NHEAD * K
    NEXP = NKEY * NKEY
    NE = NEXP // P
    NPAIR = NE // 2
    NSIM = 2 * NHEAD * NKEY
    BANK = 512
    GT = 16
    HG = GT // 2
    NG = P // GT
    SLOTS = NPAIR
    FILLS = 12
    NEG = -3.0e38
    assert NT == 2 and ND == 2 and NPICK * 2 == P and NKEY * 2 == P and SLOTS == 2 * NG

    Z_SCALE = 2.0**10
    FULL = 2.0**14
    PICK_SCALE = 2.0**13
    HEADROOM = 2.0**-11
    ONE_OVER = 2130706432.0
    EXPONENT = 0x7F800000

    C_NORM, C_FRONT, C_SEARCH, C_PICK, C_HOT, C_FINAL = 16, 23, 64, 78, 16, 4

    es = ExitStack()
    with es:

        def sb(name, shape, dt=F32):
            return es.enter_context(nc.sbuf_tensor(name, shape, dt))

        def sem(name):
            return es.enter_context(nc.semaphore(name))

        down_t = sb("down_t", [P, 2, ND, NEXP], F16)
        up = sb("up", [P, NE, 2, D], F16)
        keys_q = sb("keys_q", [P, 2, ND, NSIM], F16)
        wqk = sb("wqk", [P, ND, D])
        wv = sb("wv", [P, ND, D])
        gelu_scale = sb("gelu_scale", [P, NE])
        s_scale = sb("s_scale", [P, 1])
        out_scale = sb("out_scale", [P, 1])
        ident = sb("ident", [P, P])
        ident16 = sb("ident16", [P, P], F16)
        col = sb("col", [P, P, GT], F16)
        causal = sb("causal", [P, 3 * P], mybir.dt.bfloat16)
        s_all = sb("s_all", [P, 2, NE, NTOK])
        sims = sb("sims", [P, NT, NSIM])
        z16 = sb("z16", [P, 3, 2, ND, NTOK], F16)
        x1 = sb("x1", [P, 3, NT, D])
        x_in = sb("x_in", [P, NT, D])
        normed = sb("normed", [P, NT, D])
        normed_t = sb("normed_t", [P, ND, NTOK])
        ctx_t = sb("ctx_t", [P, ND, NTOK])
        q_t = sb("q_t", [P, ND, NTOK])
        ctx_in = q_t
        v = sb("v", [P, NT, D])
        probs = normed_t[:].rearrange("p a t -> p (a t)")[:, 0 : 3 * P]
        probs_t = normed[:].rearrange("p t d -> p (t d)")[:, 0 : 3 * P]
        stats = sb("stats", [P, NT, 6])
        mean_var = sb("mean_var", [P, NT, 2])
        var = sb("var", [P, NT])
        rstd = sb("rstd", [P, NT])
        newton = sb("newton", [P, NT])
        neg_max = sb("neg_max", [P, NT])
        row_sum = sb("row_sum", [P, NT])
        inv_sum = sb("inv_sum", [P, NT])
        top = sb("top", [P, NT, 2, NHEAD, K])
        top_at = sb("top_at", [P, NT, 2, NHEAD, K], U16)
        top_at16 = sb("top_at16", [P, 2, NHEAD, K], F16)
        best = sb("best", [P, NHEAD, K])
        best_at = sb("best_at", [P, NHEAD * K], U16)
        rank = sb("rank", [P, 2, NPICK], U16)
        key2 = sb("key2", [P, NPICK], U16)
        key2_low = sb("key2_low", [P, NPICK], U16)
        key2_high = sb("key2_high", [P, NPICK], U16)
        wmax = sb("wmax", [P, 1])
        wexp = sb("wexp", [P, 1])
        winv = sb("winv", [P, 1])
        picks = sb("picks", [P, 4, NT, NPICK], F16)
        picks_t = sb("picks_t", [P, 4, P], F16)
        token_scale = sb("token_scale", [P, 3, NT])
        hot_a = sb("hot_a", [P, 2, P, GT], F16)
        hot_b = sb("hot_b", [P, 2, 2, NT * NE, GT], F16)
        hot_j = sb("hot_j", [P, NE, GT], F16)
        work = hot_a[:, 0].rearrange("p c t -> p (c t)")
        sums = work[:, 0:1024].bitcast(F32).rearrange("p (h a) -> p h a", h=NHEAD)
        key_of = work[:, 0:256].bitcast(F32).rearrange("p (s k) -> p s k", s=2)
        weight = work[:, 256:384].bitcast(F32)
        hit = work[:, 1024:2048].rearrange("p (s k a) -> p s k a", s=2, a=K)
        w32 = sb("w32", [P, 2, 2, NTOK])
        w_hi = sb("w_hi", [P, 2, 2, NTOK], F16)
        w_lo = sb("w_lo", [P, 2, 2, NTOK], F16)

        down_in, up_in = s_all[:, 0, :, :], s_all[:, 1, :, :]
        spare = up[:, :, :, :].rearrange("p a b c -> p (a b c)").bitcast(F32)
        ffn_wq_in = spare[:, 0:4096].rearrange("p (g d) -> p g d", d=D)
        keys_in = spare[:, 4096:5120].rearrange("p (s g c) -> p s g c", s=2, c=DK)
        keys_t = spare[:, 5120:6144].rearrange("p (s k) -> p s k", s=2)
        attn_in = spare[:, 6144:7168].rearrange("p (w a d) -> p w a d", w=2, a=ND)
        attn_t = spare[:, 7168:8192].rearrange("p (w a d) -> p w a d", w=2, a=ND)
        norm_row = w32[:, 0, 0, :]
        keys_raw = sims[:]
        setup_room = w_lo[:, 1, :, :].rearrange("p e t -> p (e t)").bitcast(F32)
        norm_col, up_max, all_max = (setup_room[:, 2 * i : 2 * i + 2] for i in range(3))
        key_max, key_scale, key_exp, up_scale, up_exp = (setup_room[:, 6 + i : 7 + i] for i in range(5))
        row_max = w_lo[:, 0, 0, :].bitcast(F32)[:, 0:NE]
        row_scale = w_lo[:, 0, 1, :].bitcast(F32)[:, 0:NE]

        bank = [es.enter_context(nc.psum_tensor(f"bank{i}", [P, BANK], F32)) for i in range(8)]
        acc = bank[0:2]
        h_ps = bank[2:4]
        s_ps = bank[4:6]
        f_ps = bank[6:8]

        attn_loaded = sem("attn_loaded")
        wv_loaded = sem("wv_loaded")
        keys_loaded = sem("keys_loaded")
        down_loaded = sem("down_loaded")
        up_loaded = sem("up_loaded")
        consts = sem("consts")
        attn_turned = sem("attn_turned")
        attn_t_ready = sem("attn_t_ready")
        wqk_made = sem("wqk_made")
        wqk_ready = sem("wqk_ready")
        keys_turned = sem("keys_turned")
        keys_t_ready = sem("keys_t_ready")
        keys_made = sem("keys_made")
        keys_raw_ready = sem("keys_raw_ready")
        key_max_ready = sem("key_max_ready")
        key_max_shared = sem("key_max_shared")
        keys_q_ready = sem("keys_q_ready")
        down_normed = sem("down_normed")
        down_scaled = sem("down_scaled")
        down_turned = sem("down_turned")
        down_hi_ready = sem("down_hi_ready")
        down_lo_ready = sem("down_lo_ready")
        experts_max_ready = sem("experts_max_ready")
        experts_max_shared = sem("experts_max_shared")
        scales_ready = sem("scales_ready")
        up_hi_ready = sem("up_hi_ready")
        up_lo_ready = sem("up_lo_ready")
        setup_pool = sem("setup_pool")
        setup_dve = sem("setup_dve")
        settled = sem("settled")
        x_loaded = sem("x_loaded")
        ctx_loaded = sem("ctx_loaded")
        front_filled = sem("front_filled")
        normed_ready = sem("normed_ready")
        copied = sem("copied")
        scores_masked = sem("scores_masked")
        probs_ready = sem("probs_ready")
        x1_ready = sem("x1_ready")
        z_ready = sem("z_ready")
        z_lo_ready = sem("z_lo_ready")
        sims_used = sem("sims_used")
        dve_front = sem("dve_front")
        dve_norm = sem("dve_norm")
        dve_search = sem("dve_search")
        picks_ready = sem("picks_ready")
        picks_turned = sem("picks_turned")
        picks_t_ready = sem("picks_t_ready")
        hot_ready = sem("hot_ready")
        s_filled = sem("s_filled")
        s_stored = sem("s_stored")
        dve_pick = sem("dve_pick")
        dve_hot = sem("dve_hot")
        h_filled = sem("h_filled")
        gelu_ready = sem("gelu_ready")
        w_ready = sem("w_ready")
        w_hi_ready = sem("w_hi_ready")
        w_lo_ready = sem("w_lo_ready")
        up_done = sem("up_done")
        dve_final = sem("dve_final")
        out_ready = sem("out_ready")
        out_stored = sem("out_stored")

        COPIES = ["ctx_t", "normed_t", "v", "q_t", "probs_t", "z_hi", "sim0", "sim1", "sim2", "sim3"]
        NCOPY = len(COPIES)

        def copy_no(b, name):
            return b * NCOPY + COPIES.index(name) + 1

        def after(eng, semaphore, count):
            if isinstance(count, int) and count <= 0:
                return
            eng.wait_ge(semaphore, count)

        def settle(eng):
            eng.sem_inc(settled, 1)

        class Steps:

            def __init__(self, eng, semaphore, start=0):
                self.eng, self.semaphore, self.start, self.n = eng, semaphore, start, 0

            def add(self, instruction):
                instruction.then_inc(self.semaphore, 1)
                self.n += 1

            def met(self):
                self.eng.wait_ge(self.semaphore, self.start + self.n)

            def link(self, instruction):
                self.add(instruction)
                self.met()

        STAGES = dict(front=(0, NBATCH), following=(0, NBATCH - 1), pick=(1, NBATCH + 1), dense=(2, NBATCH + 2),
                      tail=(3, NBATCH + 3))

        def passes(eng, body, extra=lambda it: None):

            def peeled(its):
                for it in its:
                    body(it, {s for s, (a, z) in STAGES.items() if a <= it < z})
                    extra(it)

            peeled(range(0, 3))
            with eng.Fori(3, NBATCH - 1) as it:
                body(it, set(STAGES))
            peeled(range(NBATCH - 1, NBATCH + 3))

        def lagged(stages, k, lag):
            return "dense" in stages if k >= lag else "tail" in stages

        def flat(t):
            return t.rearrange("p a d -> p (a d)")

        block = es.enter_context(nc.Block())

        @block.sync
        def _(sp):
            def weight(dst, src, semaphore):
                sp.dma_start(dst, src).then_inc(semaphore, 16)

            def halves(w):
                return w.rearrange("(a p) n -> p a n", p=P)

            weight(attn_in[:, 0], halves(attn_wq), attn_loaded)
            weight(attn_in[:, 1], halves(attn_wk), attn_loaded)
            sp.dma_start(x_in[:], x[0].rearrange("(t p) d -> p t d", p=P)).then_inc(x_loaded, 16)
            sp.dma_start(ctx_in[:], ctx[0].rearrange("(t p) d -> p t d", p=P)).then_inc(ctx_loaded, 16)
            weight(wv[:], halves(attn_wv), wv_loaded)
            kv = ffn_keys.rearrange("(g h) k s c -> (h k) s g c", h=2)
            for s in range(2):
                weight(keys_in[:, s], kv[:, s], keys_loaded)
            weight(ffn_wq_in, ffn_wq.rearrange("(g p) d -> p g d", p=P), keys_loaded)
            sp.dma_start(norm_col, norm_w.rearrange("(a p) -> p a", p=P),
                         allow_slow_non_contiguous=True).then_inc(keys_loaded, 16)
            weight(norm_row, norm_w.partition_broadcast(P), down_loaded)
            for w, src, semaphore in ((down_in, expert_down, down_loaded), (up_in, expert_up, up_loaded)):
                for a in range(2):
                    weight(w[a * NKEY : (a + 1) * NKEY],
                           src.rearrange("(i j2 jp) d -> jp i j2 d", j2=NE, jp=2)[a], semaphore)

            def load_x(b):
                after(sp, x1_ready, b)
                sp.dma_start(x_in[:], x[b].rearrange("(t p) d -> p t d", p=P)).then_inc(x_loaded, 16)

            def load_ctx(b):
                after(sp, front_filled, (b - 1) * FILLS + 5 if not isinstance(b, int) or b > 0 else 0)
                sp.dma_start(ctx_in[:], ctx[b].rearrange("(t p) d -> p t d", p=P)).then_inc(ctx_loaded, 16)

            def body(it, stages):
                if "tail" in stages:
                    sp.wait_ge(out_ready, it - 2)
                    sp.dma_start(
                        out[it - 3].rearrange("(t p) d -> p t d", p=P), x1[:, it % 3, :, :]
                    ).then_inc(out_stored, 16)
                if "front" in stages and not (isinstance(it, int) and it == NBATCH - 1):
                    load_ctx(it + 1)
                    load_x(it + 1)

            for it in range(0, 3):
                body(it, {"front"})
            with sp.Fori(3, NBATCH - 1) as it:
                body(it, {"front", "tail"})
            for it in range(NBATCH - 1, NBATCH + 3):
                body(it, {"tail"})
            sp.wait_ge(out_stored, 16 * NBATCH)

        @block.gpsimd
        def _(pool):
            st = Steps(pool, setup_pool)
            st.add(nc.gpsimd.memset(ident[:], 0.0))
            st.add(nc.gpsimd.memset(ident16[:], 0.0))
            st.add(nc.gpsimd.memset(causal[:], 0.0))
            st.add(nc.gpsimd.memset(hot_b[:].rearrange("p a b c t -> p (a b c t)"), 0.0))
            st.add(nc.gpsimd.iota(col[:], [[1, P], [0, GT]], base=0, channel_multiplier=0,
                                  allow_small_or_imprecise_dtypes=True))
            st.met()
            for m in (ident, ident16):
                st.add(nc.gpsimd.affine_select(out=m[:], in_=m[:], compare_op=ALU.not_equal, fill=1.0, base=0,
                                               pattern=[[-1, P]], channel_multiplier=1))
            for c in (0, 2 * P):
                st.add(nc.gpsimd.affine_select(out=causal[:, c : c + P], in_=causal[:, c : c + P],
                                               compare_op=ALU.is_ge, fill=NEG, base=0,
                                               pattern=[[-1, P]], channel_multiplier=1))
            st.met()
            nc.gpsimd.memset(newton[:], 0.0).then_inc(consts, 1)
            rmax = bass.bass_isa.ReduceOp.max
            pool.wait_ge(key_max_ready, 1)
            nc.gpsimd.partition_all_reduce(key_scale, key_max, P, rmax).then_inc(key_max_shared, 1)
            pool.wait_ge(down_loaded, 16 * 3)
            nc.gpsimd.tensor_tensor(down_in, down_in, norm_row.unsqueeze(1).to_broadcast([P, NE, D]),
                                    ALU.mult).then_inc(down_normed, 1)
            pool.wait_ge(experts_max_ready, 1)
            nc.gpsimd.partition_all_reduce(all_max, up_max, P, rmax).then_inc(experts_max_shared, 1)
            pool.wait_ge(up_hi_ready, 2)
            nc.gpsimd.tensor_tensor(up[:, :, 1, :], up_in, up[:, :, 0, :], ALU.subtract).then_inc(up_lo_ready, 1)

            def body(it, stages):
                for k in range(SLOTS):
                    n = (it - 2) * NPAIR + k
                    if "dense" in stages:
                        if k == 0:
                            pool.wait_ge(s_stored, (it - 1) * NG)
                        pool.wait_ge(gelu_ready, n + 1)
                        nc.gpsimd.tensor_tensor(w32[:, k % 2], w32[:, k % 2], s_all[:, it % 2, 2 * k : 2 * k + 2, :],
                                                ALU.mult).then_inc(w_ready, 1)
                    if lagged(stages, k, 1):
                        pool.wait_ge(w_hi_ready, n)
                        after(pool, up_done, n - 2)
                        nc.gpsimd.tensor_tensor(w_lo[:, (k - 1) % 2], w32[:, (k - 1) % 2], w_hi[:, (k - 1) % 2],
                                                ALU.subtract).then_inc(w_lo_ready, 1)

            passes(pool, body)

        @block.scalar
        def _(act):
            act.wait_ge(attn_turned, 1)
            for w in range(2):
                nc.scalar.activation(flat(attn_t[:, w]), bank[w][:], ACT.Copy).then_inc(attn_t_ready, 1)
            act.wait_ge(wqk_made, 1)
            nc.scalar.activation(flat(wqk[:]), bank[2][:], ACT.Copy, scale=float(D) ** -0.5).then_inc(wqk_ready, 1)
            act.wait_ge(keys_turned, 1)
            for s in range(2):
                nc.scalar.activation(keys_t[:, s], bank[4 + s][:], ACT.Copy).then_inc(keys_t_ready, 1)

            def copy(dst, src, **kw):
                nc.scalar.activation(dst, src, ACT.Copy, **kw).then_inc(copied, 1)

            def body(it, stages):
                for k in range(SLOTS):
                    n = (it - 2) * NPAIR + k
                    if "dense" in stages:
                        act.wait_ge(h_filled, n + 1)
                        after(act, w_lo_ready, n - 1)
                        after(act, w_hi_ready, n - 1)
                        for e in range(2):
                            g = nc.scalar.activation(w32[:, k % 2, e, :], h_ps[k % 2][:, e * NTOK : (e + 1) * NTOK],
                                                     ACT.Gelu, scale=gelu_scale[:, 2 * k + e : 2 * k + e + 1])
                        g.then_inc(gelu_ready, 1)
                    if lagged(stages, k, 1):
                        act.wait_ge(w_ready, n)
                        after(act, up_done, n - 2)
                        nc.scalar.activation(w_hi[:, (k - 1) % 2], w32[:, (k - 1) % 2], ACT.Copy).then_inc(w_hi_ready, 1)
                    if "front" in stages:
                        b = it

                        def filled(i):
                            act.wait_ge(front_filled, b * FILLS + i + 1)

                        if k == 0:
                            filled(0)
                            copy(flat(ctx_t[:]), f_ps[0][:])
                            filled(1)
                            copy(flat(normed_t[:]), f_ps[1][:])
                        if k == 1:
                            filled(2)
                            copy(flat(v[:]), f_ps[0][:])
                            filled(3)
                            copy(flat(q_t[:]), f_ps[1][:])
                        if k == 2:
                            act.wait_ge(scores_masked, b + 1)
                            for t, cols in ((0, slice(0, P)), (1, slice(P, 3 * P))):
                                nc.scalar.activation(probs[:, cols], probs[:, cols], ACT.Exp, bias=neg_max[:, t : t + 1],
                                                     accum_out=row_sum[:, t : t + 1]).then_inc(probs_ready, 1)
                        if k == 4:
                            filled(5)
                            copy(probs_t, f_ps[1][:, 0 : 3 * P])
                        if k == 7:
                            filled(7)
                            after(act, h_filled, (it - 2) * NPAIR)
                            copy(flat(z16[:, it % 3, 0]), f_ps[1][:])
                        if 8 <= k < 12:
                            i = k - 8
                            filled(8 + i)
                            after(act, sims_used, (b - 1) * NT + i // 2 + 1 if not isinstance(b, int) or b > 0 else 0)
                            copy(sims[:, i // 2, (i % 2) * BANK : (i % 2 + 1) * BANK], f_ps[i % 2][:])
                    if "pick" in stages:
                        b = it - 1
                        if k == NG - 2:
                            act.wait_ge(picks_turned, b + 1)
                            after(act, hot_ready, b * NG * NT)
                            nc.scalar.activation(picks_t[:].rearrange("p q t -> p (q t)"),
                                                 s_ps[0][:].bitcast(F16)[:, 0 : 4 * P], ACT.Copy).then_inc(picks_t_ready, 1)
                        if k >= NG:
                            g = k - NG
                            if g == 0:
                                after(act, w_ready, (b - 1) * NPAIR)
                            act.wait_ge(s_filled, b * NG + g + 1)
                            tiles = s_all[:, (it + 1) % 2].rearrange("p j (t n) -> p t j n", t=NT)
                            for half in range(2):
                                at = g * GT + half * HG
                                s = nc.scalar.activation(
                                    tiles[:, :, :, at : at + HG],
                                    s_ps[half][:].rearrange("p (t j n) -> p t j n", t=NT, n=HG), ACT.Copy,
                                    scale=s_scale[:, 0:1])
                            s.then_inc(s_stored, 1)

            def experts(it):
                if it != 0:
                    return
                for g in range(NE * ND // 4):
                    a, q = g % ND, g // ND
                    act.wait_ge(down_turned, g + 1)
                    nc.scalar.activation(down_t[:, 0, a, q * BANK : (q + 1) * BANK], bank[g % 4][:],
                                         ACT.Copy).then_inc(down_hi_ready, 1)
                act.wait_ge(scales_ready, 1)
                rows = up_in.rearrange("p a b -> p (a b)")
                nc.scalar.activation(rows, rows, ACT.Copy, scale=up_scale[:, 0:1]).then_inc(up_hi_ready, 1)
                act.wait_ge(up_hi_ready, 1)
                nc.scalar.activation(up[:, :, 0, :], up_in, ACT.Copy).then_inc(up_hi_ready, 1)

            passes(act, body, experts)

        @block.vector
        def _(dve):
            st = Steps(dve, setup_dve)

            def ts(o, i, s1, s2, op0, op1=None):
                return nc.vector.tensor_scalar(o, i, s1, s2, op0, op1) if op1 is not None else nc.vector.tensor_scalar(
                    o, i, s1, s2, op0)

            def power_of_two(o, i, steps):
                steps.link(ts(o.bitcast(I32), i.bitcast(I32), EXPONENT, None, ALU.bitwise_and))

            def inverse(o, i, steps):
                steps.link(ts(o.bitcast(I32), i.bitcast(I32), -1.0, ONE_OVER, ALU.mult, ALU.add))

            def keys():
                dve.wait_ge(keys_made, 1)
                for a in range(ND):
                    for s in range(2):
                        st.add(ts(keys_raw[:, a, s * BANK : (s + 1) * BANK], bank[2 * a + s][:], norm_col[:, a : a + 1],
                                  None, ALU.mult))
                st.met()
                dve.sem_inc(keys_raw_ready, 1)
                nc.vector.tensor_reduce(key_max, flat(keys_raw), X, ALU.max,
                                        apply_absolute_value=True).then_inc(key_max_ready, 1)
                dve.wait_ge(key_max_shared, 1)
                st.link(ts(key_scale, key_scale, 1e-30, None, ALU.max))
                power_of_two(key_exp, key_scale, st)
                inverse(key_scale, key_exp, st)
                st.link(ts(flat(keys_raw), flat(keys_raw), key_scale, FULL, ALU.mult, ALU.mult))
                st.link(nc.vector.tensor_copy(keys_q[:, 0], keys_raw))
                nc.vector.tensor_tensor(keys_q[:, 1], keys_raw, keys_q[:, 0], ALU.subtract).then_inc(keys_q_ready, 1)

            def up_largest():
                dve.wait_ge(up_loaded, 16 * 2)
                st.add(nc.vector.tensor_reduce(up_max[:, 1:2], flat(up_in), X, ALU.max, apply_absolute_value=True))

            def experts(it):
                if it != 0:
                    return
                dve.wait_ge(down_normed, 1)
                st.link(nc.vector.tensor_reduce(row_max, down_in, X, ALU.max, apply_absolute_value=True))
                st.link(nc.vector.tensor_reduce(up_max[:, 0:1], row_max, X, ALU.max))
                dve.sem_inc(experts_max_ready, 1)
                st.link(ts(row_max, row_max, 1e-30, None, ALU.max))
                power_of_two(row_scale, row_max, st)
                st.add(ts(gelu_scale[:], row_scale, 1.0 / (FULL * Z_SCALE), None, ALU.mult))
                inverse(row_max, row_scale, st)
                for j in range(NE):
                    ts(down_in[:, j, :], down_in[:, j, :], row_max[:, j : j + 1], FULL, ALU.mult,
                       ALU.mult).then_inc(down_scaled, 1)
                dve.wait_ge(experts_max_shared, 1)
                st.link(ts(all_max, all_max, 1e-30, None, ALU.max))
                power_of_two(all_max, all_max, st)
                inverse(up_scale, all_max[:, 1:2], st)
                st.link(ts(up_scale, up_scale, FULL, None, ALU.mult))
                dve.sem_inc(scales_ready, 1)
                st.link(ts(up_exp, all_max[:, 1:2], 1.0 / FULL, None, ALU.mult))
                inverse(s_scale[:], all_max[:, 0:1], st)
                st.link(ts(s_scale[:], s_scale[:], HEADROOM, None, ALU.mult))
                st.link(ts(out_scale[:], all_max[:, 0:1], up_exp, 1.0 / (PICK_SCALE * HEADROOM), ALU.mult, ALU.mult))
                st.link(ts(out_scale[:], out_scale[:], key_exp, 1.0 / (FULL * Z_SCALE), ALU.mult, ALU.mult))
                for g in range(NE * ND // 4):
                    a, q = g % ND, g // ND
                    cols = slice(q * BANK, (q + 1) * BANK)
                    dve.wait_ge(down_hi_ready, g + 1)
                    nc.vector.tensor_tensor(down_t[:, 1, a, cols], bank[g % 4][:], down_t[:, 0, a, cols],
                                            ALU.subtract).then_inc(down_lo_ready, 1)

            def normalise(src, steps, factor, eps, scale, ready):
                for t in range(NT):
                    steps.add(nc.vector.bn_stats(stats[:, t, :], src(t)))
                steps.met()
                settle(dve)
                for t in range(NT):
                    steps.add(nc.vector.bn_aggr(mean_var[:, t, :], stats[:, t, :]))
                steps.met()
                steps.link(ts(var[:], mean_var[:, :, 1], factor, eps, ALU.mult, ALU.add))
                steps.link(ts(rstd[:].bitcast(I32), var[:].bitcast(I32), 1, None, ALU.logical_shift_right))
                steps.link(ts(rstd[:].bitcast(I32), rstd[:].bitcast(I32), -1.0, float(0x5F3759DF), ALU.mult, ALU.add))
                for _ in range(3):
                    steps.link(nc.vector.tensor_tensor(newton[:], rstd[:], rstd[:], ALU.mult))
                    steps.link(nc.vector.scalar_tensor_tensor(newton[:], newton[:], -0.5, var[:], ALU.mult, ALU.mult))
                    steps.link(nc.vector.scalar_tensor_tensor(rstd[:], newton[:], 1.5, rstd[:], ALU.add, ALU.mult))
                if scale != 1.0:
                    steps.link(ts(rstd[:], rstd[:], scale, None, ALU.mult))
                for t in range(NT):
                    last = ts(normed[:, t, :], src(t), mean_var[:, t, 0:1], rstd[:, t : t + 1], ALU.subtract, ALU.mult)
                    last.then_inc(ready, 1)

            def layernorm_x(b):
                steps = Steps(dve, dve_norm, b * C_NORM)
                dve.wait_ge(x_loaded, 16 * (b + 1))
                after(dve, front_filled, (b - 1) * FILLS + 8 if not isinstance(b, int) or b > 0 else 0)
                normalise(lambda t: x_in[:, t, :], steps, 1.0, 1e-5, 1.0, normed_ready)
                assert steps.n == C_NORM, steps.n

            def search(t, at, b):
                steps = Steps(dve, dve_search, b * C_SEARCH + (2 * t + at) * 2 * NHEAD)
                if not at:
                    dve.wait_ge(copied, copy_no(b, "sim1" if t == 0 else "sim3"))
                    if t == 0:
                        after(dve, picks_ready, NT * b)
                else:
                    steps.met()
                settle(dve)
                for s in range(2):
                    for h in range(NHEAD):
                        c = (s * NHEAD + h) * NKEY
                        if at:
                            steps.add(nc.vector.max_index(top_at[:, t, s, h, :], top[:, t, s, h, :], sims[:, t, c : c + NKEY]))
                        else:
                            steps.add(nc.vector.max(top[:, t, s, h, :], sims[:, t, c : c + NKEY]))
                if at:
                    steps.met()
                    dve.sem_inc(sims_used, 1)

            def best_sums(t, b, pick):
                if t == 0:
                    after(dve, s_filled, b * NG)
                pick.add(nc.vector.tensor_copy(top_at16[:], top_at[:, t]))
                pick.link(nc.vector.tensor_tensor(
                    sums.rearrange("p h (a b) -> p h a b", a=K),
                    top[:, t, 0].unsqueeze(3).to_broadcast([P, NHEAD, K, K]),
                    top[:, t, 1].unsqueeze(2).to_broadcast([P, NHEAD, K, K]), ALU.add))
                settle(dve)
                for h in range(NHEAD):
                    pick.add(nc.vector.max(best[:, h, :], sums[:, h, :]))
                pick.met()
                settle(dve)
                for h in range(NHEAD):
                    pick.add(nc.vector.max_index(best_at[:, h * K : (h + 1) * K], best[:, h, :], sums[:, h, :]))
                pick.met()

            def encode(t, b, it, pick):
                pick.add(ts(rank[:, 0], best_at[:], 3, None, ALU.logical_shift_right))
                pick.link(ts(rank[:, 1], best_at[:], K - 1, None, ALU.bitwise_and))
                for s in range(2):
                    pick.add(nc.vector.tensor_tensor(
                        hit[:, s], rank[:, s].unsqueeze(2).to_broadcast([P, NPICK, K]),
                        col[:, 0:K, 0].unsqueeze(1).to_broadcast([P, NPICK, K]), ALU.is_equal))
                pick.add(nc.vector.tensor_reduce(wmax[:], best[:, :, 0], X, ALU.max))
                pick.met()
                for s in range(2):
                    h4 = hit[:, s].rearrange("p (h k) a -> p h k a", k=K)
                    pick.add(nc.vector.tensor_tensor(
                        h4, h4, top_at16[:, s].unsqueeze(2).to_broadcast([P, NHEAD, K, K]), ALU.mult))
                pick.add(ts(wmax[:], wmax[:], 1e-30, 1e30, ALU.max, ALU.min))
                pick.met()
                pick.add(nc.vector.tensor_reduce(key_of, hit, X, ALU.add))
                power_of_two(wexp[:], wmax[:], pick)
                pick.add(nc.vector.tensor_copy(key2[:], key_of[:, 1]))
                inverse(winv[:], wexp[:], pick)
                pick.add(ts(key2_low[:], key2[:], 1, None, ALU.bitwise_and))
                pick.add(ts(key2_high[:], key2[:], 1, None, ALU.logical_shift_right))
                pick.link(ts(winv[:], winv[:], PICK_SCALE, None, ALU.mult))
                if t == 0:
                    after(dve, picks_turned, b)
                pick.add(ts(weight, best[:].rearrange("p h k -> p (h k)"), 0.0, winv[:], ALU.max, ALU.mult))
                pick.add(ts(token_scale[:, (it + 2) % 3, t : t + 1], wexp[:], out_scale[:], None, ALU.mult))
                pick.add(nc.vector.scalar_tensor_tensor(picks[:, 0, t, :], key2_low[:], float(NKEY),
                                                        key_of[:, 0], ALU.mult, ALU.add))
                pick.add(nc.vector.tensor_copy(picks[:, 1, t, :], key2_high[:]))
                pick.met()
                pick.link(nc.vector.tensor_copy(picks[:, 2, t, :], weight))
                pick.link(nc.vector.tensor_tensor(picks[:, 3, t, :], weight, picks[:, 2, t, :], ALU.subtract))
                dve.sem_inc(picks_ready, 1)

            def one_hot(g, b, hot):
                if g == 0:
                    dve.wait_ge(picks_t_ready, b + 1)
                after(dve, s_filled, b * NG + g - 1)
                cols = slice(g * GT, (g + 1) * GT)
                hot.add(nc.vector.tensor_tensor(
                    hot_a[:, g % 2], picks_t[:, 0, cols].unsqueeze(1).to_broadcast([P, P, GT]), col[:], ALU.is_equal))
                after(dve, hot_ready, (b * NG + g) * NT)
                hot.add(nc.vector.tensor_tensor(
                    hot_j[:], picks_t[:, 1, cols].unsqueeze(1).to_broadcast([P, NE, GT]), col[:, 0:NE, :], ALU.is_equal))
                hot.met()
                for t in range(NT):
                    rows = slice(t * NPICK, (t + 1) * NPICK)
                    nc.vector.tensor_tensor(
                        hot_b[rows, g % 2, :, t * NE : (t + 1) * NE, :],
                        hot_j[rows].unsqueeze(1).to_broadcast([NPICK, 2, NE, GT]),
                        picks_t[rows, 2:4, cols].unsqueeze(2).to_broadcast([NPICK, 2, NE, GT]),
                        ALU.mult).then_inc(hot_ready, 1)

            def body(it, stages):
                front = Steps(dve, dve_front, it * C_FRONT)
                pick = Steps(dve, dve_pick, (it - 1) * C_PICK)
                hot = Steps(dve, dve_hot, (it - 1) * C_HOT)
                fin = Steps(dve, dve_final, (it - 3) * C_FINAL)
                for k in range(SLOTS):
                    if "tail" in stages and k == 2:
                        dve.wait_ge(up_done, (it - 2) * NPAIR)
                        for half in range(2):
                            for t in range(NT):
                                o = x1[:, it % 3, t, :]
                                fin.add(nc.vector.scalar_tensor_tensor(
                                    o, acc[t][:, half * D : (half + 1) * D], token_scale[:, it % 3, t : t + 1], o,
                                    ALU.mult, ALU.add))
                            fin.met()
                        dve.sem_inc(out_ready, 1)
                    if "pick" in stages:
                        b = it - 1
                        if k in (0, 3):
                            best_sums(k // 3, b, pick)
                        if k in (1, 4):
                            encode(k // 3, b, it, pick)
                        if NG - 1 <= k < 2 * NG - 1:
                            one_hot(k - (NG - 1), b, hot)
                    if "front" in stages:
                        b = it
                        if k == 2:
                            dve.wait_ge(front_filled, b * FILLS + 5)
                            after(dve, front_filled, (b - 1) * FILLS + 6 if not isinstance(b, int) or b > 0 else 0)
                            front.link(nc.vector.tensor_tensor(probs, f_ps[0][:, 0 : 3 * P], causal[:], ALU.add))
                            front.add(nc.vector.tensor_reduce(neg_max[:, 0:1], probs[:, 0:P], X, ALU.max, negate=True))
                            front.link(nc.vector.tensor_reduce(neg_max[:, 1:2], probs[:, P : 3 * P], X, ALU.max,
                                                               negate=True))
                            dve.sem_inc(scores_masked, 1)
                        if k == 5:
                            dve.wait_ge(probs_ready, 2 * (b + 1))
                            front.link(nc.vector.reciprocal(inv_sum[:], row_sum[:]))
                            dve.wait_ge(front_filled, b * FILLS + 7)
                            after(dve, out_stored, (it - 2) * 16)
                            for t in range(NT):
                                front.add(nc.vector.scalar_tensor_tensor(
                                    x1[:, it % 3, t, :], f_ps[0][:, t * D : (t + 1) * D], inv_sum[:, t : t + 1],
                                    x_in[:, t, :], ALU.mult, ALU.add))
                            front.met()
                            dve.sem_inc(x1_ready, 1)
                            normalise(lambda t: x1[:, it % 3, t, :], front, 1.0 + 1e-6, 1e-11, Z_SCALE, z_ready)
                        if k == 7:
                            dve.wait_ge(copied, copy_no(b, "z_hi"))
                            after(dve, h_filled, (it - 2) * NPAIR)
                            nc.vector.tensor_tensor(flat(z16[:, it % 3, 1]), f_ps[1][:], flat(z16[:, it % 3, 0]),
                                                    ALU.subtract).then_inc(z_lo_ready, 1)
                        if isinstance(it, int) and it == 0 and k == 8:
                            up_largest()
                        if k in (10, 11):
                            search(0, k == 11, b)
                        if k in (13, 14):
                            search(1, k == 14, b)
                    if "following" in stages and k == SLOTS - 1:
                        layernorm_x(it + 1)
                for name, steps, count, stage in (("front", front, C_FRONT, "front"), ("pick", pick, C_PICK, "pick"),
                                                  ("hot", hot, C_HOT, "pick"), ("final", fin, C_FINAL, "tail")):
                    assert steps.n == (count if stage in stages else 0), (name, steps.n)

            dve.wait_ge(consts, 1)
            layernorm_x(0)
            keys()
            passes(dve, body, experts)

        @block.tensor
        def _(pe):
            mm, turn = nc.tensor.matmul, nc.tensor.transpose
            pe.wait_ge(attn_loaded, 16 * 2)
            pe.wait_ge(consts, 1)
            for w in range(2):
                for a in range(ND):
                    for c in range(ND):
                        t = turn(bank[w][:, c * D + a * P : c * D + (a + 1) * P], attn_in[:, w, a, c * P : (c + 1) * P],
                                 ident[:])
            t.then_inc(attn_turned, 1)
            pe.wait_ge(attn_t_ready, 2)
            for a in range(ND):
                for c in range(ND):
                    t = mm(bank[2][:, a * D : (a + 1) * D], attn_t[:, 0, c, a * P : (a + 1) * P], attn_t[:, 1, c, :],
                           start=(c == 0), stop=(c == ND - 1))
            t.then_inc(wqk_made, 1)
            pe.wait_ge(keys_loaded, 16 * 4)
            for s in range(2):
                for g in range(NHEAD // 2):
                    t = turn(bank[4 + s][:, g * P : (g + 1) * P], keys_in[:, s, g, :], ident[:])
            t.then_inc(keys_turned, 1)
            pe.wait_ge(wqk_ready, 1)
            pe.wait_ge(keys_t_ready, 2)
            for a in range(ND):
                for s in range(2):
                    for h in range(NHEAD):
                        t = mm(bank[2 * a + s][:, h * NKEY : (h + 1) * NKEY],
                               ffn_wq_in[:, 2 * h + s, a * P : (a + 1) * P], keys_t[:, s, h * NKEY : (h + 1) * NKEY],
                               start=True, stop=True)
            t.then_inc(keys_made, 1)
            pe.wait_ge(wv_loaded, 16)

            def experts(it):
                if it == 1:
                    pe.wait_ge(up_lo_ready, 1)
                if it != 0:
                    return
                pe.wait_ge(keys_raw_ready, 1)
                for g in range(NE * ND // 4):
                    a, q = g % ND, g // ND
                    pe.wait_ge(down_scaled, 4 * (q + 1))
                    after(pe, down_lo_ready, g - 3)
                    for i in range(4):
                        t = turn(bank[g % 4][:, i * P : (i + 1) * P], down_in[:, 4 * q + i, a * P : (a + 1) * P], ident[:])
                    t.then_inc(down_turned, 1)
                pe.wait_ge(down_lo_ready, NE * ND // 4)

            def body(it, stages):
                for k in range(SLOTS):
                    n = (it - 2) * NPAIR + k
                    if "dense" in stages:
                        if k == 0:
                            pe.wait_ge(z_lo_ready, it - 1)
                        after(pe, gelu_ready, n - 1)
                        for e in range(2):
                            j = 2 * k + e
                            terms = [(gp, zp, a) for gp, a in ((0, 0), (0, 1), (1, 0), (1, 1)) for zp in range(2 - gp)]
                            for i, (gp, zp, a) in enumerate(terms):
                                h = mm(h_ps[k % 2][:, e * NTOK : (e + 1) * NTOK], down_t[:, gp, a, j * P : (j + 1) * P],
                                       z16[:, (it + 1) % 3, zp, a, :], start=(i == 0), stop=(i == len(terms) - 1))
                        h.then_inc(h_filled, 1)
                    if "front" in stages:
                        front(it, k)
                    if "pick" in stages:
                        b = it - 1
                        if k == NG - 2:
                            pe.wait_ge(picks_ready, NT * (b + 1))
                            after(pe, s_stored, b * NG)
                            turned = s_ps[0][:].bitcast(F16)
                            for q in range(4):
                                t = turn(turned[:, q * P : (q + 1) * P], picks[:, q].rearrange("p t k -> p (t k)"),
                                         ident16[:])
                            t.then_inc(picks_turned, 1)
                        if k >= NG:
                            g = k - NG
                            pe.wait_ge(hot_ready, (b * NG + g + 1) * NT)
                            if g == 0:
                                pe.wait_ge(picks_t_ready, b + 1)
                            else:
                                pe.wait_ge(s_stored, b * NG + g)
                            for i in range(GT):
                                o = s_ps[i // HG][:].rearrange("p (j t) -> p j t", t=HG)
                                for part in range(2):
                                    m = mm(o[:, :, i % HG], hot_a[:, g % 2, :, i], hot_b[:, g % 2, part, :, i],
                                           start=(part == 0), stop=(part == 1))
                            m.then_inc(s_filled, 1)
                    if lagged(stages, k, 2):
                        j = (k - 2) % NPAIR
                        pe.wait_ge(w_hi_ready, n - 1)
                        pe.wait_ge(w_lo_ready, n - 1)
                        if j == 0:
                            after(pe, out_ready, it - 2)
                        for t in range(NT):
                            for e in range(2):
                                cols = slice(t * P, (t + 1) * P)
                                mm(acc[t][:, 0 : 2 * D], w_hi[:, j % 2, e, cols],
                                   up[:, 2 * j + e].rearrange("p q d -> p (q d)"),
                                   start=(j == 0 and e == 0), stop=False)
                                u = mm(acc[t][:, 0:D], w_lo[:, j % 2, e, cols], up[:, 2 * j + e, 0, :],
                                       start=False, stop=(j == NPAIR - 1 and e == 1))
                        u.then_inc(up_done, 1)

            def front(b, k):
                def fill(m):
                    m.then_inc(front_filled, 1)

                def turn_tiles(dst, src):
                    for a in range(ND):
                        for t in range(NT):
                            m = turn(dst[:, a * NTOK + t * P : a * NTOK + (t + 1) * P], src[:, t, a * P : (a + 1) * P],
                                     ident[:])
                    fill(m)

                def from_(name):
                    pe.wait_ge(copied, copy_no(b, name))

                if k == 0:
                    pe.wait_ge(ctx_loaded, 16 * (b + 1))
                    after(pe, copied, copy_no(b - 1, "sim2") if not isinstance(b, int) or b > 0 else 0)
                    turn_tiles(f_ps[0], ctx_in)
                    pe.wait_ge(normed_ready, NT * (b + 1))
                    after(pe, copied, copy_no(b - 1, "sim3") if not isinstance(b, int) or b > 0 else 0)
                    turn_tiles(f_ps[1], normed)
                if k == 1:
                    from_("ctx_t")
                    for t in range(NT):
                        for a in range(ND):
                            m = mm(f_ps[0][:, t * D : (t + 1) * D], ctx_t[:, a, t * P : (t + 1) * P], wv[:, a, :],
                                   start=(a == 0), stop=(a == ND - 1))
                    fill(m)
                    from_("normed_t")
                    for c in range(ND):
                        for a in range(ND):
                            m = mm(f_ps[1][:, c * NTOK : (c + 1) * NTOK], wqk[:, a, c * P : (c + 1) * P],
                                   normed_t[:, a, :], start=(a == 0), stop=(a == ND - 1))
                    fill(m)
                if k == 2:
                    from_("q_t")
                    for t in range(NT):
                        for a in range(ND):
                            m = mm(f_ps[0][:, t * P : (2 * t + 1) * P], q_t[:, a, t * P : (t + 1) * P],
                                   ctx_t[:, a, 0 : (t + 1) * P], start=(a == 0), stop=(a == ND - 1))
                    fill(m)
                if k == 4:
                    pe.wait_ge(probs_ready, 2 * (b + 1))
                    for i in range(3):
                        m = turn(f_ps[1][:, i * P : (i + 1) * P], probs[:, i * P : (i + 1) * P], ident[:])
                    fill(m)
                if k == 5:
                    from_("probs_t")
                    for t, blocks in ((0, (0,)), (1, (1, 2))):
                        for i, c in enumerate(blocks):
                            m = mm(f_ps[0][:, t * D : (t + 1) * D], probs_t[:, c * P : (c + 1) * P], v[:, i, :],
                                   start=(i == 0), stop=(i == len(blocks) - 1))
                    fill(m)
                if k == 7:
                    pe.wait_ge(z_ready, NT * (b + 1))
                    turn_tiles(f_ps[1], normed)
                if 8 <= k < 12:
                    i = k - 8
                    t, c = i // 2, i % 2
                    if i == 0:
                        if isinstance(b, int) and b == 0:
                            pe.wait_ge(keys_q_ready, 1)
                        from_("z_hi")
                        pe.wait_ge(z_lo_ready, b + 1)
                    else:
                        from_(f"sim{i - 2}") if i >= 2 else None
                    terms = [(zp, kp, a) for a in range(ND) for zp, kp in ((0, 0), (0, 1), (1, 0))]
                    for j, (zp, kp, a) in enumerate(terms):
                        m = mm(f_ps[c][:, :], z16[:, b % 3, zp, a, t * P : (t + 1) * P],
                               keys_q[:, kp, a, c * BANK : (c + 1) * BANK], start=(j == 0), stop=(j == len(terms) - 1))
                    fill(m)

            passes(pe, body, experts)


_INS = ["x", "ctx_1024", "L0_xattn_w_q", "L0_xattn_w_k", "L0_xattn_w_v", "L0_ffn_w_q", "L0_ffn_keys",
        "L0_ffn_expert_down", "L0_ffn_expert_up", "L0_ffn_norm_w"]


def kernel(**inputs):
    import numpy as np
    import concourse.bacc as bacc
    from concourse.bass_utils import run_bass_kernel_spmd

    nc = bacc.Bacc("TRN2", target_bir_lowering=False, num_devices=1)
    arrays, args = {}, []
    for name in _INS:
        a = np.ascontiguousarray(inputs[name])
        arrays[f"in_{name}"] = a
        args.append(nc.dram_tensor(f"in_{name}", a.shape, mybir.dt.from_np(a.dtype), kind="ExternalInput").ap())
    shape = arrays["in_x"].shape
    args.append(nc.dram_tensor("out_dram", shape, mybir.dt.float32, kind="ExternalOutput").ap())
    cross_attention_and_expert_ffn(nc, *args)
    return run_bass_kernel_spmd(nc, [arrays], core_ids=[0]).results[0]["out_dram"]
```

```python
from contextlib import ExitStack

import concourse.bass as bass
from concourse import mybir


def cross_attention_and_expert_ffn(
    nc: bass.Bass,
    x: bass.AP,
    ctx: bass.AP,
    attn_wq: bass.AP,
    attn_wk: bass.AP,
    attn_wv: bass.AP,
    ffn_wq: bass.AP,
    ffn_keys: bass.AP,
    expert_down: bass.AP,
    expert_up: bass.AP,
    norm_w: bass.AP,
    out: bass.AP,
):
    F32, F16 = mybir.dt.float32, mybir.dt.float16
    U16, I32 = mybir.dt.uint16, mybir.dt.int32
    ALU = mybir.AluOpType
    ACT = mybir.ActivationFunctionType
    X = mybir.AxisListType.X

    P = 128
    NBATCH, NTOK, D = x.shape
    NT = NTOK // P
    ND = D // P
    NHEAD, NKEY, _, DK = ffn_keys.shape
    K = 8
    NPICK = NHEAD * K
    NEXP = NKEY * NKEY
    NE = NEXP // P
    NPAIR = NE // 2
    NSIM = 2 * NHEAD * NKEY
    BANK = 512
    GT = 16
    HG = GT // 2
    NG = P // GT
    SLOTS = NPAIR
    TURN_AT = 5
    S_AT = (8, 9, 10, 11, 12, 13, 14, 15)
    NCHUNK = 4
    UP_LAG = 3
    UP_AT = 5
    HOT_AT = (6, 7, 8, 9, 10, 11, 12, 13)
    FILLS = 12
    NEG = -3.0e38
    assert NT == 2 and ND == 2 and NPICK * 2 == P and NKEY * 2 == P and SLOTS == 2 * NG

    Z_SCALE = 2.0**10
    FULL = 2.0**14
    PICK_SCALE = 2.0**13
    HEADROOM = 2.0**-11
    ONE_OVER = 2130706432.0
    EXPONENT = 0x7F800000

    C_NORM, C_FRONT, C_SEARCH, C_PICK, C_HOT, C_FINAL = 16, 22, 64, 54, 16, 4

    es = ExitStack()
    with es:

        def sb(name, shape, dt=F32):
            return es.enter_context(nc.sbuf_tensor(name, shape, dt))

        def sem(name):
            return es.enter_context(nc.semaphore(name))

        down_t = sb("down_t", [P, 2, ND, NEXP], F16)
        up = sb("up", [P, NE, 2, D], F16)
        keys_q = sb("keys_q", [P, 2, ND, NSIM], F16)
        wqk = sb("wqk", [P, ND, D])
        wv = sb("wv", [P, ND, D])
        gelu_scale = sb("gelu_scale", [P, NE])
        s_scale = sb("s_scale", [P, 1])
        out_scale = sb("out_scale", [P, 1])
        ident = sb("ident", [P, P])
        ident16 = sb("ident16", [P, P], F16)
        col = sb("col", [P, P, GT], F16)
        causal = sb("causal", [P, 3 * P], mybir.dt.bfloat16)
        s_all = sb("s_all", [P, 2, NE, NTOK])
        sims = sb("sims", [P, NT, NSIM])
        z16 = sb("z16", [P, 3, 2, ND, NTOK], F16)
        x1 = sb("x1", [P, 3, NT, D])
        x_in = sb("x_in", [P, NT, D])
        normed = sb("normed", [P, NT, D])
        normed_t = sb("normed_t", [P, ND, NTOK])
        ctx_t = sb("ctx_t", [P, ND, NTOK])
        q_t = sb("q_t", [P, ND, NTOK])
        ctx_in = q_t
        v = ctx_t
        probs = normed_t[:].rearrange("p a t -> p (a t)")[:, 0 : 3 * P]
        probs_t = normed[:].rearrange("p t d -> p (t d)")[:, 0 : 3 * P]
        stats = sb("stats", [P, NT, 6])
        mean_var = sb("mean_var", [P, NT, 2])
        var = sb("var", [P, NT])
        rstd = sb("rstd", [P, NT])
        newton = sb("newton", [P, NT])
        neg_max = sb("neg_max", [P, NT])
        row_sum = sb("row_sum", [P, NT])
        inv_sum = sb("inv_sum", [P, NT])
        top = sb("top", [P, 2, NT, NHEAD, K])
        top_at = sb("top_at", [P, 2, NT, NHEAD, K], U16)
        best = sb("best", [P, NT, NHEAD, K])
        wmax = sb("wmax", [P, NT])
        wexp = sb("wexp", [P, NT])
        winv = sb("winv", [P, NT])
        picks = sb("picks", [P, 4, NT, NPICK], F16)
        picks_t = sb("picks_t", [P, 4, P], F16)
        token_scale = sb("token_scale", [P, 3, NT])
        hot_a = sb("hot_a", [P, 2, P, GT], F16)
        hot_b = sb("hot_b", [P, 2, 2, NT * NE, GT], F16)
        hot_j = sb("hot_j", [P, NE, GT], F16)
        work = hot_a[:, 0].rearrange("p c t -> p (c t)")
        sums = work.bitcast(F32).rearrange("p (t h a) -> p t h a", t=NT, h=NHEAD)
        top_at16 = work[:, 0:256].rearrange("p (s t h k) -> p s t h k", s=2, t=NT, h=NHEAD)
        weight = work[:, 256:512].bitcast(F32)
        key_of = work[:, 512:768].bitcast(U16).rearrange("p (s n) -> p s n", s=2)
        hit = hot_a[:, 1].rearrange("p c t -> p (c t)").rearrange("p (n a) -> p n a", a=K)
        numbers = hot_j[:].rearrange("p c t -> p (c t)").bitcast(U16)
        best_at = numbers[:, 0:128].rearrange("p (t h k) -> p t h k", t=NT, h=NHEAD)
        rank = numbers[:, 128:384].rearrange("p (s n) -> p s n", s=2)
        key2_low, key2_high = rank[:, 0], rank[:, 1]
        gelu = sb("gelu", [P, 2, NTOK])
        w32 = sb("w32", [P, 2, 2, NTOK])
        w_hi = sb("w_hi", [P, 2, 2, NTOK], F16)
        w_lo = sb("w_lo", [P, 2, 2, NTOK], F16)

        down_in, up_in = s_all[:, 0, :, :], s_all[:, 1, :, :]
        spare = up[:, :, :, :].rearrange("p a b c -> p (a b c)").bitcast(F32)
        ffn_wq_in = spare[:, 0:4096].rearrange("p (g d) -> p g d", d=D)
        keys_in = spare[:, 4096:5120].rearrange("p (s g c) -> p s g c", s=2, c=DK)
        keys_t = spare[:, 5120:6144].rearrange("p (s k) -> p s k", s=2)
        attn_in = spare[:, 6144:7168].rearrange("p (w a d) -> p w a d", w=2, a=ND)
        attn_t = spare[:, 7168:8192].rearrange("p (w a d) -> p w a d", w=2, a=ND)
        norm_row = w32[:, 0, 0, :]
        keys_raw = sims[:]
        setup_room = w_lo[:, 1, :, :].rearrange("p e t -> p (e t)").bitcast(F32)
        norm_col, up_max, all_max = (setup_room[:, 2 * i : 2 * i + 2] for i in range(3))
        key_max, key_scale, key_exp, up_scale, up_exp = (setup_room[:, 6 + i : 7 + i] for i in range(5))
        up_halves = setup_room[:, 12:14]
        row_max = w_lo[:, 0, 0, :].bitcast(F32)[:, 0:NE]
        row_scale = w_lo[:, 0, 1, :].bitcast(F32)[:, 0:NE]

        bank = [es.enter_context(nc.psum_tensor(f"bank{i}", [P, BANK], F32)) for i in range(8)]
        acc = bank[0:2]
        h_ps = bank[2:4]
        s_ps = bank[4:6]
        f_ps = bank[6:8]

        attn_loaded = sem("attn_loaded")
        wv_loaded = sem("wv_loaded")
        keys_loaded = sem("keys_loaded")
        down_loaded = sem("down_loaded")
        up_loaded = sem("up_loaded")
        consts = sem("consts")
        attn_turned = sem("attn_turned")
        attn_t_ready = sem("attn_t_ready")
        wqk_made = sem("wqk_made")
        wqk_ready = sem("wqk_ready")
        keys_turned = sem("keys_turned")
        keys_t_ready = sem("keys_t_ready")
        keys_made = sem("keys_made")
        keys_raw_ready = sem("keys_raw_ready")
        key_max_ready = sem("key_max_ready")
        key_max_shared = sem("key_max_shared")
        key_scale_ready = sem("key_scale_ready")
        keys_hi_ready = sem("keys_hi_ready")
        keys_q_ready = sem("keys_q_ready")
        down_normed = sem("down_normed")
        row_scale_ready = sem("row_scale_ready")
        up_scaled = sem("up_scaled")
        down_scaled = sem("down_scaled")
        down_turned = sem("down_turned")
        down_hi_ready = sem("down_hi_ready")
        down_lo_ready = sem("down_lo_ready")
        experts_max_ready = sem("experts_max_ready")
        experts_max_shared = sem("experts_max_shared")
        scales_ready = sem("scales_ready")
        up_hi_ready = sem("up_hi_ready")
        up_lo_ready = sem("up_lo_ready")
        setup_pool = sem("setup_pool")
        setup_dve = sem("setup_dve")
        settled = sem("settled")
        x_loaded = sem("x_loaded")
        ctx_loaded = sem("ctx_loaded")
        front_filled = sem("front_filled")
        normed_ready = sem("normed_ready")
        copied = sem("copied")
        scores_masked = sem("scores_masked")
        probs_ready = sem("probs_ready")
        x1_ready = sem("x1_ready")
        z_ready = sem("z_ready")
        z_lo_ready = sem("z_lo_ready")
        sims_used = sem("sims_used")
        dve_front = sem("dve_front")
        dve_norm = sem("dve_norm")
        dve_search = sem("dve_search")
        picks_ready = sem("picks_ready")
        picks_turned = sem("picks_turned")
        picks_t_ready = sem("picks_t_ready")
        hot_ready = sem("hot_ready")
        s_filled = sem("s_filled")
        s_stored = sem("s_stored")
        dve_pick = sem("dve_pick")
        dve_hot = sem("dve_hot")
        h_filled = sem("h_filled")
        gelu_ready = sem("gelu_ready")
        w_ready = sem("w_ready")
        w_hi_ready = sem("w_hi_ready")
        w_lo_ready = sem("w_lo_ready")
        w_lo_late = sem("w_lo_late")
        up_done = sem("up_done")
        dve_final = sem("dve_final")
        out_ready = sem("out_ready")
        out_stored = sem("out_stored")

        COPIES = ["ctx_t", "normed_t", "q_t", "v", "probs_t", "z_hi", "sim0", "sim1", "sim2", "sim3"]
        NCOPY = len(COPIES)

        def copy_no(b, name):
            return b * NCOPY + COPIES.index(name) + 1

        def after(eng, semaphore, count):
            if isinstance(count, int) and count <= 0:
                return
            eng.wait_ge(semaphore, count)

        def settle(eng):
            eng.sem_inc(settled, 1)

        class Steps:

            def __init__(self, eng, semaphore, start=0):
                self.eng, self.semaphore, self.start, self.n = eng, semaphore, start, 0

            def add(self, instruction):
                instruction.then_inc(self.semaphore, 1)
                self.n += 1

            def met(self):
                self.eng.wait_ge(self.semaphore, self.start + self.n)

            def link(self, instruction):
                self.add(instruction)
                self.met()

        STAGES = dict(front=(0, NBATCH), following=(0, NBATCH - 1), pick=(1, NBATCH + 1), dense=(2, NBATCH + 2),
                      tail=(3, NBATCH + 3))

        def passes(eng, body, extra=lambda it: None):

            def peeled(its):
                for it in its:
                    body(it, {s for s, (a, z) in STAGES.items() if a <= it < z})
                    extra(it)

            peeled(range(0, 3))
            with eng.Fori(3, NBATCH - 1) as it:
                body(it, set(STAGES))
            peeled(range(NBATCH - 1, NBATCH + 3))

        LATE = (NBATCH - 1) * NPAIR - 1

        def low_part(engine, eng, it, k):
            n = (it - 2) * NPAIR + k
            eng.wait_ge(w_hi_ready, n)
            after(eng, up_done, n - 2)
            engine.tensor_tensor(w_lo[:, (k - 1) % 2], w32[:, (k - 1) % 2], w_hi[:, (k - 1) % 2],
                                 ALU.subtract).then_inc(w_lo_late if front_over(it) else w_lo_ready, 1)

        def after_low_part(eng, it, k, lag):
            pair = (it - 2) * NPAIR + k - lag
            if isinstance(it, int) and pair >= LATE:
                eng.wait_ge(w_lo_late, pair - LATE + 1)
            else:
                after(eng, w_lo_ready, pair + 1)

        def front_over(it):
            return isinstance(it, int) and it > NBATCH

        def lagged(stages, k, lag):
            return "dense" in stages if k >= lag else "tail" in stages

        def flat(t):
            return t.rearrange("p a d -> p (a d)")

        block = es.enter_context(nc.Block())

        @block.sync
        def _(sp):
            def weight(dst, src, semaphore):
                sp.dma_start(dst, src).then_inc(semaphore, 16)

            def halves(w):
                return w.rearrange("(a p) n -> p a n", p=P)

            weight(attn_in[:, 0], halves(attn_wq), attn_loaded)
            weight(attn_in[:, 1], halves(attn_wk), attn_loaded)
            sp.dma_start(x_in[:], x[0].rearrange("(t p) d -> p t d", p=P)).then_inc(x_loaded, 16)
            sp.dma_start(ctx_in[:], ctx[0].rearrange("(t p) d -> p t d", p=P)).then_inc(ctx_loaded, 16)
            weight(wv[:], halves(attn_wv), wv_loaded)
            kv = ffn_keys.rearrange("(g h) k s c -> (h k) s g c", h=2)
            for s in range(2):
                weight(keys_in[:, s], kv[:, s], keys_loaded)
            weight(ffn_wq_in, ffn_wq.rearrange("(g p) d -> p g d", p=P), keys_loaded)
            sp.dma_start(norm_col, norm_w.rearrange("(a p) -> p a", p=P),
                         allow_slow_non_contiguous=True).then_inc(keys_loaded, 16)
            weight(norm_row, norm_w.partition_broadcast(P), down_loaded)
            for w, src, semaphore in ((down_in, expert_down, down_loaded), (up_in, expert_up, up_loaded)):
                for a in range(2):
                    weight(w[a * NKEY : (a + 1) * NKEY],
                           src.rearrange("(i j2 jp) d -> jp i j2 d", j2=NE, jp=2)[a], semaphore)

            def load_x(b):
                after(sp, x1_ready, b)
                sp.dma_start(x_in[:], x[b].rearrange("(t p) d -> p t d", p=P)).then_inc(x_loaded, 16)

            def load_ctx(b):
                after(sp, front_filled, (b - 1) * FILLS + 4 if not isinstance(b, int) or b > 0 else 0)
                sp.dma_start(ctx_in[:], ctx[b].rearrange("(t p) d -> p t d", p=P)).then_inc(ctx_loaded, 16)

            def body(it, stages):
                if "tail" in stages:
                    sp.wait_ge(out_ready, it - 2)
                    sp.dma_start(
                        out[it - 3].rearrange("(t p) d -> p t d", p=P), x1[:, it % 3, :, :]
                    ).then_inc(out_stored, 16)
                if "front" in stages and not (isinstance(it, int) and it == NBATCH - 1):
                    load_ctx(it + 1)
                    load_x(it + 1)

            for it in range(0, 3):
                body(it, {"front"})
            with sp.Fori(3, NBATCH - 1) as it:
                body(it, {"front", "tail"})
            for it in range(NBATCH - 1, NBATCH + 3):
                body(it, {"tail"})
            sp.wait_ge(out_stored, 16 * NBATCH)

        @block.gpsimd
        def _(pool):
            st = Steps(pool, setup_pool)
            st.add(nc.gpsimd.memset(ident[:], 0.0))
            st.add(nc.gpsimd.memset(ident16[:], 0.0))
            st.add(nc.gpsimd.memset(causal[:], 0.0))
            st.add(nc.gpsimd.memset(hot_b[:].rearrange("p a b c t -> p (a b c t)"), 0.0))
            st.add(nc.gpsimd.iota(col[:], [[1, P], [0, GT]], base=0, channel_multiplier=0,
                                  allow_small_or_imprecise_dtypes=True))
            st.met()
            for m in (ident, ident16):
                st.add(nc.gpsimd.affine_select(out=m[:], in_=m[:], compare_op=ALU.not_equal, fill=1.0, base=0,
                                               pattern=[[-1, P]], channel_multiplier=1))
            for c in (0, 2 * P):
                st.add(nc.gpsimd.affine_select(out=causal[:, c : c + P], in_=causal[:, c : c + P],
                                               compare_op=ALU.is_ge, fill=NEG, base=0,
                                               pattern=[[-1, P]], channel_multiplier=1))
            st.met()
            nc.gpsimd.memset(newton[:], 0.0).then_inc(consts, 1)
            rmax = bass.bass_isa.ReduceOp.max
            pool.wait_ge(down_loaded, 16 * 3)
            for i in range(NCHUNK):
                if i == NCHUNK - 1:
                    pool.wait_ge(key_max_ready, 1)
                    nc.gpsimd.partition_all_reduce(key_scale, key_max, P, rmax).then_inc(key_max_shared, 1)
                tiles = slice(i * NE // NCHUNK, (i + 1) * NE // NCHUNK)
                nc.gpsimd.tensor_tensor(down_in[:, tiles], down_in[:, tiles],
                                        norm_row.unsqueeze(1).to_broadcast([P, NE // NCHUNK, D]),
                                        ALU.mult).then_inc(down_normed, 1)
            pool.wait_ge(experts_max_ready, 1)
            nc.gpsimd.partition_all_reduce(all_max, up_max, P, rmax).then_inc(experts_max_shared, 1)
            pool.wait_ge(scales_ready, 1)
            nc.gpsimd.tensor_tensor(up_in, up_in, up_scale.unsqueeze(1).to_broadcast([P, NE, D]),
                                    ALU.mult).then_inc(up_scaled, 1)
            for i in range(NG):
                tiles = slice(i * NE // NG, (i + 1) * NE // NG)
                pool.wait_ge(up_hi_ready, i + 1)
                nc.gpsimd.tensor_tensor(up[:, tiles, 1, :], up_in[:, tiles], up[:, tiles, 0, :],
                                        ALU.subtract).then_inc(up_lo_ready, 1)

            def body(it, stages):
                for k in range(SLOTS):
                    n = (it - 2) * NPAIR + k
                    if "dense" in stages:
                        if k == 0:
                            pool.wait_ge(s_stored, (it - 1) * NG)
                        pool.wait_ge(gelu_ready, n + 1)
                        after_low_part(pool, it, k, 2)
                        after(pool, w_hi_ready, n - 1)
                        nc.gpsimd.tensor_tensor(w32[:, k % 2], gelu[:], s_all[:, it % 2, 2 * k : 2 * k + 2, :],
                                                ALU.mult).then_inc(w_ready, 1)
                    if lagged(stages, k, 1) and not front_over(it):
                        low_part(nc.gpsimd, pool, it, k)

            passes(pool, body)

        @block.scalar
        def _(act):
            act.wait_ge(attn_turned, 1)
            for w in range(2):
                nc.scalar.activation(flat(attn_t[:, w]), bank[w][:], ACT.Copy).then_inc(attn_t_ready, 1)
            act.wait_ge(wqk_made, 1)
            nc.scalar.activation(flat(wqk[:]), bank[2][:], ACT.Copy, scale=float(D) ** -0.5).then_inc(wqk_ready, 1)
            def copy(dst, src, **kw):
                nc.scalar.activation(dst, src, ACT.Copy, **kw).then_inc(copied, 1)

            def body(it, stages):
                for k in range(SLOTS):
                    n = (it - 2) * NPAIR + k
                    if "dense" in stages:
                        act.wait_ge(h_filled, n + 1)
                        after(act, w_ready, n)
                        for e in range(2):
                            g = nc.scalar.activation(gelu[:, e, :], h_ps[k % 2][:, e * NTOK : (e + 1) * NTOK],
                                                     ACT.Gelu, scale=gelu_scale[:, 2 * k + e : 2 * k + e + 1])
                        g.then_inc(gelu_ready, 1)
                    if lagged(stages, k, 1) and k >= S_AT[0]:
                        act.wait_ge(w_ready, n)
                        after(act, up_done, n - 2)
                        nc.scalar.activation(w_hi[:, (k - 1) % 2], w32[:, (k - 1) % 2], ACT.Copy).then_inc(w_hi_ready, 1)
                    if "pick" in stages:
                        b = it - 1
                        if k == TURN_AT:
                            act.wait_ge(picks_turned, b + 1)
                            after(act, hot_ready, b * NG * NT)
                            nc.scalar.activation(picks_t[:].rearrange("p q t -> p (q t)"),
                                                 s_ps[0][:].bitcast(F16)[:, 0 : 4 * P], ACT.Copy).then_inc(picks_t_ready, 1)
                        if k in S_AT:
                            g = S_AT.index(k)
                            if g == 0:
                                after(act, w_ready, (b - 1) * NPAIR)
                            act.wait_ge(s_filled, b * NG + g + 1)
                            tiles = s_all[:, (it + 1) % 2].rearrange("p j (t n) -> p t j n", t=NT)
                            for half in range(2):
                                at = g * GT + half * HG
                                s = nc.scalar.activation(
                                    tiles[:, :, :, at : at + HG],
                                    s_ps[half][:].rearrange("p (t j n) -> p t j n", t=NT, n=HG), ACT.Copy,
                                    scale=s_scale[:, 0:1])
                            s.then_inc(s_stored, 1)
                    if "front" in stages:
                        b = it

                        def filled(i):
                            act.wait_ge(front_filled, b * FILLS + i + 1)

                        if k == 0:
                            filled(0)
                            copy(flat(ctx_t[:]), f_ps[0][:])
                            filled(1)
                            copy(flat(normed_t[:]), f_ps[1][:])
                        if k == 1:
                            filled(2)
                            copy(flat(q_t[:]), f_ps[1][:])
                        if k == 3:
                            act.wait_ge(scores_masked, b + 1)
                            for t, cols in ((0, slice(0, P)), (1, slice(P, 3 * P))):
                                nc.scalar.activation(probs[:, cols], probs[:, cols], ACT.Exp, bias=neg_max[:, t : t + 1],
                                                     accum_out=row_sum[:, t : t + 1]).then_inc(probs_ready, 1)
                            filled(4)
                            copy(flat(v[:]), f_ps[1][:])
                            if isinstance(it, int) and it == 0:
                                act.wait_ge(keys_turned, 1)
                                for s in range(2):
                                    nc.scalar.activation(keys_t[:, s], bank[4 + s][:], ACT.Copy).then_inc(keys_t_ready, 1)
                        if k == 4:
                            filled(5)
                            copy(probs_t, f_ps[0][:, 0 : 3 * P])
                        if isinstance(it, int) and it == 0 and k == 5:
                            act.wait_ge(keys_made, 1)
                            for a in range(ND):
                                for s in range(2):
                                    nc.scalar.activation(keys_raw[:, a, s * BANK : (s + 1) * BANK], bank[2 * a + s][:],
                                                         ACT.Copy, scale=norm_col[:, a : a + 1]).then_inc(keys_raw_ready, 1)
                            act.wait_ge(key_scale_ready, 1)
                            nc.scalar.activation(keys_q[:, 0], keys_raw, ACT.Copy,
                                                 scale=key_scale).then_inc(keys_hi_ready, 1)
                        if k == 7:
                            filled(7)
                            after(act, h_filled, (it - 2) * NPAIR)
                            copy(flat(z16[:, it % 3, 0]), f_ps[1][:], scale=Z_SCALE)
                        if 8 <= k < 12:
                            i = k - 8
                            filled(8 + i)
                            after(act, sims_used, (b - 1) * NT + i // 2 + 1 if not isinstance(b, int) or b > 0 else 0)
                            copy(sims[:, i // 2, (i % 2) * BANK : (i % 2 + 1) * BANK], f_ps[i % 2][:])
                    if lagged(stages, k, 1) and k < S_AT[0]:
                        act.wait_ge(w_ready, n)
                        after(act, up_done, n - 2)
                        nc.scalar.activation(w_hi[:, (k - 1) % 2], w32[:, (k - 1) % 2], ACT.Copy).then_inc(w_hi_ready, 1)
                    if isinstance(it, int) and it == 1 and UP_AT <= k < UP_AT + NG:
                        i = k - UP_AT
                        tiles = slice(i * NE // NG, (i + 1) * NE // NG)
                        act.wait_ge(up_scaled, 1)
                        nc.scalar.activation(up[:, tiles, 0, :], up_in[:, tiles], ACT.Copy).then_inc(up_hi_ready, 1)

            def experts(it):
                if it != 0:
                    return
                act.wait_ge(row_scale_ready, 1)
                for q in range(NE // 4 + 1):
                    if q < NE // 4:
                        for j in range(4 * q, 4 * q + 4):
                            nc.scalar.activation(down_in[:, j, :], down_in[:, j, :], ACT.Copy,
                                                 scale=row_max[:, j : j + 1]).then_inc(down_scaled, 1)
                    if q > 0:
                        for a in range(ND):
                            g = (q - 1) * ND + a
                            act.wait_ge(down_turned, g + 1)
                            nc.scalar.activation(down_t[:, 0, a, (q - 1) * BANK : q * BANK], bank[g % 8][:],
                                                 ACT.Copy).then_inc(down_hi_ready, 1)

            passes(act, body, experts)

        @block.vector
        def _(dve):
            st = Steps(dve, setup_dve)

            def ts(o, i, s1, s2, op0, op1=None):
                return nc.vector.tensor_scalar(o, i, s1, s2, op0, op1) if op1 is not None else nc.vector.tensor_scalar(
                    o, i, s1, s2, op0)

            def power_of_two(o, i, steps):
                steps.link(ts(o.bitcast(I32), i.bitcast(I32), EXPONENT, None, ALU.bitwise_and))

            def inverse(o, i, steps):
                steps.link(ts(o.bitcast(I32), i.bitcast(I32), -1.0, ONE_OVER, ALU.mult, ALU.add))

            def keys():
                dve.wait_ge(keys_raw_ready, 2 * ND)
                nc.vector.tensor_reduce(key_max, flat(keys_raw), X, ALU.max,
                                        apply_absolute_value=True).then_inc(key_max_ready, 1)
                up_largest(0)
                dve.wait_ge(key_max_shared, 1)
                st.link(ts(key_scale, key_scale, 1e-30, None, ALU.max))
                power_of_two(key_exp, key_scale, st)
                inverse(key_scale, key_exp, st)
                st.link(ts(key_scale, key_scale, FULL, None, ALU.mult))
                dve.sem_inc(key_scale_ready, 1)
                down_largest(0)
                dve.wait_ge(keys_hi_ready, 1)
                nc.vector.scalar_tensor_tensor(keys_q[:, 1], keys_raw, key_scale, keys_q[:, 0], ALU.mult,
                                               ALU.subtract).then_inc(keys_q_ready, 1)

            def down_largest(i):
                tiles = slice(i * NE // NCHUNK, (i + 1) * NE // NCHUNK)
                dve.wait_ge(down_normed, i + 1)
                st.add(nc.vector.tensor_reduce(row_max[:, tiles], down_in[:, tiles], X, ALU.max,
                                               apply_absolute_value=True))

            def down_scales():
                for i in range(1, NCHUNK):
                    down_largest(i)
                st.met()
                st.add(nc.vector.tensor_reduce(up_max[:, 0:1], row_max, X, ALU.max))
                st.link(ts(row_max, row_max, 1e-30, None, ALU.max))
                power_of_two(row_scale, row_max, st)
                st.add(ts(gelu_scale[:], row_scale, 1.0 / (FULL * Z_SCALE), None, ALU.mult))
                inverse(row_max, row_scale, st)
                st.link(ts(row_max, row_max, FULL, None, ALU.mult))
                dve.sem_inc(row_scale_ready, 1)

            def up_largest(half):
                dve.wait_ge(up_loaded, 16 * 2)
                tiles = slice(half * NE // 2, (half + 1) * NE // 2)
                st.add(nc.vector.tensor_reduce(up_halves[:, half : half + 1], flat(up_in[:, tiles]), X, ALU.max,
                                               apply_absolute_value=True))
                if half == 1:
                    st.met()
                    st.link(nc.vector.tensor_reduce(up_max[:, 1:2], up_halves, X, ALU.max))
                    dve.sem_inc(experts_max_ready, 1)

            def experts(it):
                if it != 0:
                    return
                dve.wait_ge(experts_max_shared, 1)
                st.link(ts(all_max, all_max, 1e-30, None, ALU.max))
                power_of_two(all_max, all_max, st)
                inverse(up_scale, all_max[:, 1:2], st)
                st.link(ts(up_scale, up_scale, FULL, None, ALU.mult))
                dve.sem_inc(scales_ready, 1)
                st.link(ts(up_exp, all_max[:, 1:2], 1.0 / FULL, None, ALU.mult))
                inverse(s_scale[:], all_max[:, 0:1], st)
                st.link(ts(s_scale[:], s_scale[:], HEADROOM, None, ALU.mult))
                st.link(ts(out_scale[:], all_max[:, 0:1], up_exp, 1.0 / (PICK_SCALE * HEADROOM), ALU.mult, ALU.mult))
                st.link(ts(out_scale[:], out_scale[:], key_exp, 1.0 / (FULL * Z_SCALE), ALU.mult, ALU.mult))
                for g in range(NE * ND // 4):
                    a, q = g % ND, g // ND
                    cols = slice(q * BANK, (q + 1) * BANK)
                    dve.wait_ge(down_hi_ready, g + 1)
                    nc.vector.tensor_tensor(down_t[:, 1, a, cols], bank[g % 8][:], down_t[:, 0, a, cols],
                                            ALU.subtract).then_inc(down_lo_ready, 1)

            def normalise(src, steps, factor, eps, ready):
                for t in range(NT):
                    steps.add(nc.vector.bn_stats(stats[:, t, :], src(t)))
                steps.met()
                settle(dve)
                for t in range(NT):
                    steps.add(nc.vector.bn_aggr(mean_var[:, t, :], stats[:, t, :]))
                steps.met()
                steps.link(ts(var[:], mean_var[:, :, 1], factor, eps, ALU.mult, ALU.add))
                steps.link(ts(rstd[:].bitcast(I32), var[:].bitcast(I32), 1, None, ALU.logical_shift_right))
                steps.link(ts(rstd[:].bitcast(I32), rstd[:].bitcast(I32), -1.0, float(0x5F3759DF), ALU.mult, ALU.add))
                for _ in range(3):
                    steps.link(nc.vector.tensor_tensor(newton[:], rstd[:], rstd[:], ALU.mult))
                    steps.link(nc.vector.scalar_tensor_tensor(newton[:], newton[:], -0.5, var[:], ALU.mult, ALU.mult))
                    steps.link(nc.vector.scalar_tensor_tensor(rstd[:], newton[:], 1.5, rstd[:], ALU.add, ALU.mult))
                for t in range(NT):
                    last = ts(normed[:, t, :], src(t), mean_var[:, t, 0:1], rstd[:, t : t + 1], ALU.subtract, ALU.mult)
                    last.then_inc(ready, 1)

            def layernorm_x(b):
                steps = Steps(dve, dve_norm, b * C_NORM)
                dve.wait_ge(x_loaded, 16 * (b + 1))
                after(dve, front_filled, (b - 1) * FILLS + 8 if not isinstance(b, int) or b > 0 else 0)
                normalise(lambda t: x_in[:, t, :], steps, 1.0, 1e-5, normed_ready)
                assert steps.n == C_NORM, steps.n

            def search(t, at, b):
                steps = Steps(dve, dve_search, b * C_SEARCH + (2 * t + at) * 2 * NHEAD)
                if not at:
                    dve.wait_ge(copied, copy_no(b, "sim1" if t == 0 else "sim3"))
                    if t == 0:
                        after(dve, picks_ready, b)
                else:
                    steps.met()
                settle(dve)
                for s in range(2):
                    for h in range(NHEAD):
                        c = (s * NHEAD + h) * NKEY
                        if at:
                            steps.add(nc.vector.max_index(top_at[:, s, t, h, :], top[:, s, t, h, :], sims[:, t, c : c + NKEY]))
                        else:
                            steps.add(nc.vector.max(top[:, s, t, h, :], sims[:, t, c : c + NKEY]))
                if at:
                    steps.met()
                    dve.sem_inc(sims_used, 1)

            def best_sums(b, pick):
                after(dve, s_filled, b * NG)
                pairs = [P, NT * NHEAD, K, K]
                side = lambda s: top[:, s].rearrange("p t h k -> p (t h) k")
                pick.link(nc.vector.tensor_tensor(
                    sums.rearrange("p t h (a b) -> p (t h) a b", a=K), side(0).unsqueeze(3).to_broadcast(pairs),
                    side(1).unsqueeze(2).to_broadcast(pairs), ALU.add))
                settle(dve)
                for t in range(NT):
                    for h in range(NHEAD):
                        pick.add(nc.vector.max(best[:, t, h, :], sums[:, t, h, :]))
                pick.met()
                settle(dve)
                for t in range(NT):
                    for h in range(NHEAD):
                        pick.add(nc.vector.max_index(best_at[:, t, h, :], best[:, t, h, :], sums[:, t, h, :]))
                pick.met()

            def find_ranks(pick):
                at = best_at.rearrange("p t h k -> p (t h k)")
                pick.add(ts(rank[:, 0], at, 3, None, ALU.logical_shift_right))
                pick.add(ts(rank[:, 1], at, K - 1, None, ALU.bitwise_and))
                pick.add(nc.vector.tensor_copy(top_at16, top_at[:]))
                pick.met()

            def mark_ranks(pick):
                pick.add(nc.vector.tensor_tensor(
                    hit, rank.rearrange("p s n -> p (s n)").unsqueeze(2).to_broadcast([P, 2 * NT * NPICK, K]),
                    col[:, 0:K, 0].unsqueeze(1).to_broadcast([P, 2 * NT * NPICK, K]), ALU.is_equal))
                pick.add(nc.vector.tensor_reduce(wmax[:], best[:, :, :, 0], X, ALU.max))
                pick.met()

            def find_keys(pick):
                runs = [P, 2 * NT * NHEAD, K, K]
                h4 = hit.rearrange("p (g k) a -> p g k a", k=K)
                pick.add(nc.vector.tensor_tensor(
                    h4, h4, top_at16.rearrange("p s t h k -> p (s t h) k").unsqueeze(2).to_broadcast(runs), ALU.mult))
                pick.add(ts(wmax[:], wmax[:], 1e-30, 1e30, ALU.max, ALU.min))
                pick.met()
                pick.add(nc.vector.tensor_tensor(hit[:, :, 0:4], hit[:, :, 0:4], hit[:, :, 4:8], ALU.add))
                power_of_two(wexp[:], wmax[:], pick)
                pick.add(nc.vector.tensor_tensor(hit[:, :, 0:2], hit[:, :, 0:2], hit[:, :, 2:4], ALU.add))
                inverse(winv[:], wexp[:], pick)
                pick.add(nc.vector.tensor_tensor(key_of.rearrange("p s n -> p (s n)"), hit[:, :, 0], hit[:, :, 1], ALU.add))
                pick.link(ts(winv[:], winv[:], PICK_SCALE, None, ALU.mult))

            def encode(b, it, pick):
                pick.add(ts(key2_low, key_of[:, 1], 1, None, ALU.bitwise_and))
                pick.add(ts(key2_high, key_of[:, 1], 1, None, ALU.logical_shift_right))
                w3 = weight.rearrange("p (t n) -> p t n", t=NT)
                pick.add(nc.vector.scalar_tensor_tensor(
                    w3, best[:].rearrange("p t h k -> p t (h k)"), 0.0,
                    winv[:].unsqueeze(2).to_broadcast([P, NT, NPICK]), ALU.max, ALU.mult))
                pick.add(ts(token_scale[:, (it + 2) % 3, :], wexp[:], out_scale[:], None, ALU.mult))
                pick.met()
                after(dve, picks_turned, b)

                def code(q):
                    return picks[:, q].rearrange("p t k -> p (t k)")

                pick.add(nc.vector.scalar_tensor_tensor(code(0), key2_low, float(NKEY), key_of[:, 0], ALU.mult, ALU.add))
                pick.add(nc.vector.tensor_copy(code(1), key2_high))
                pick.link(nc.vector.tensor_copy(code(2), weight))
                pick.link(nc.vector.tensor_tensor(code(3), weight, code(2), ALU.subtract))
                dve.sem_inc(picks_ready, 1)

            def one_hot(g, b, hot):
                if g == 0:
                    dve.wait_ge(picks_t_ready, b + 1)
                after(dve, s_filled, b * NG + g - 1)
                cols = slice(g * GT, (g + 1) * GT)
                hot.add(nc.vector.tensor_tensor(
                    hot_a[:, g % 2], picks_t[:, 0, cols].unsqueeze(1).to_broadcast([P, P, GT]), col[:], ALU.is_equal))
                after(dve, hot_ready, (b * NG + g) * NT)
                hot.add(nc.vector.tensor_tensor(
                    hot_j[:], picks_t[:, 1, cols].unsqueeze(1).to_broadcast([P, NE, GT]), col[:, 0:NE, :], ALU.is_equal))
                hot.met()
                for t in range(NT):
                    rows = slice(t * NPICK, (t + 1) * NPICK)
                    nc.vector.tensor_tensor(
                        hot_b[rows, g % 2, :, t * NE : (t + 1) * NE, :],
                        hot_j[rows].unsqueeze(1).to_broadcast([NPICK, 2, NE, GT]),
                        picks_t[rows, 2:4, cols].unsqueeze(2).to_broadcast([NPICK, 2, NE, GT]),
                        ALU.mult).then_inc(hot_ready, 1)

            def body(it, stages):
                front = Steps(dve, dve_front, it * C_FRONT)
                pick = Steps(dve, dve_pick, (it - 1) * C_PICK)
                hot = Steps(dve, dve_hot, (it - 1) * C_HOT)
                fin = Steps(dve, dve_final, (it - 3) * C_FINAL)
                for k in range(SLOTS):
                    if "pick" in stages:
                        b = it - 1
                        if k == 0:
                            best_sums(b, pick)
                        if k == 1:
                            find_ranks(pick)
                    if lagged(stages, k, 1) and front_over(it):
                        low_part(nc.vector, dve, it, k)
                    if "pick" in stages and k == 2:
                        mark_ranks(pick)
                    if "tail" in stages and k == 2:
                        dve.wait_ge(up_done, (it - 2) * NPAIR)
                        for half in range(2):
                            for t in range(NT):
                                o = x1[:, it % 3, t, :]
                                fin.add(nc.vector.scalar_tensor_tensor(
                                    o, acc[t][:, half * D : (half + 1) * D], token_scale[:, it % 3, t : t + 1], o,
                                    ALU.mult, ALU.add))
                            fin.met()
                        dve.sem_inc(out_ready, 1)
                    if "front" in stages:
                        b = it
                        if k == 2:
                            dve.wait_ge(front_filled, b * FILLS + 4)
                            after(dve, front_filled, (b - 1) * FILLS + 6 if not isinstance(b, int) or b > 0 else 0)
                            front.link(nc.vector.tensor_tensor(probs, f_ps[0][:, 0 : 3 * P], causal[:], ALU.add))
                            front.add(nc.vector.tensor_reduce(neg_max[:, 0:1], probs[:, 0:P], X, ALU.max, negate=True))
                            front.link(nc.vector.tensor_reduce(neg_max[:, 1:2], probs[:, P : 3 * P], X, ALU.max,
                                                               negate=True))
                            dve.sem_inc(scores_masked, 1)
                    if "pick" in stages and k == 2:
                        find_keys(pick)
                        encode(it - 1, it, pick)
                    if "front" in stages:
                        b = it
                        if k == 5:
                            dve.wait_ge(probs_ready, 2 * (b + 1))
                            front.link(nc.vector.reciprocal(inv_sum[:], row_sum[:]))
                            dve.wait_ge(front_filled, b * FILLS + 7)
                            after(dve, out_stored, (it - 2) * 16)
                            for t in range(NT):
                                front.add(nc.vector.scalar_tensor_tensor(
                                    x1[:, it % 3, t, :], f_ps[1][:, t * D : (t + 1) * D], inv_sum[:, t : t + 1],
                                    x_in[:, t, :], ALU.mult, ALU.add))
                            front.met()
                            dve.sem_inc(x1_ready, 1)
                            normalise(lambda t: x1[:, it % 3, t, :], front, 1.0 + 1e-6, 1e-11, z_ready)
                        if isinstance(it, int) and it == 0 and k == 6:
                            keys()
                        if k == 7:
                            dve.wait_ge(copied, copy_no(b, "z_hi"))
                            after(dve, h_filled, (it - 2) * NPAIR)
                            nc.vector.scalar_tensor_tensor(
                                flat(z16[:, it % 3, 1]), f_ps[1][:], Z_SCALE, flat(z16[:, it % 3, 0]), ALU.mult,
                                ALU.subtract).then_inc(z_lo_ready, 1)
                        if isinstance(it, int) and it == 0 and k == 8:
                            down_scales()
                        if isinstance(it, int) and it == 0 and k == 12:
                            up_largest(1)
                        if k in (10, 11):
                            search(0, k == 11, b)
                        if k == 12:
                            search(1, False, b)
                    if "pick" in stages and k in HOT_AT:
                        one_hot(HOT_AT.index(k), it - 1, hot)
                    if "following" in stages and k == 14:
                        layernorm_x(it + 1)
                    if "front" in stages and k == 15:
                        search(1, True, it)
                for name, steps, count, stage in (("front", front, C_FRONT, "front"), ("pick", pick, C_PICK, "pick"),
                                                  ("hot", hot, C_HOT, "pick"), ("final", fin, C_FINAL, "tail")):
                    assert steps.n == (count if stage in stages else 0), (name, steps.n)

            dve.wait_ge(consts, 1)
            layernorm_x(0)
            passes(dve, body, experts)

        @block.tensor
        def _(pe):
            mm, turn = nc.tensor.matmul, nc.tensor.transpose
            pe.wait_ge(attn_loaded, 16 * 2)
            pe.wait_ge(consts, 1)
            for w in range(2):
                for a in range(ND):
                    for c in range(ND):
                        t = turn(bank[w][:, c * D + a * P : c * D + (a + 1) * P], attn_in[:, w, a, c * P : (c + 1) * P],
                                 ident[:])
            t.then_inc(attn_turned, 1)
            pe.wait_ge(attn_t_ready, 2)
            for a in range(ND):
                for c in range(ND):
                    t = mm(bank[2][:, a * D : (a + 1) * D], attn_t[:, 0, c, a * P : (a + 1) * P], attn_t[:, 1, c, :],
                           start=(c == 0), stop=(c == ND - 1))
            t.then_inc(wqk_made, 1)
            pe.wait_ge(wqk_ready, 1)
            pe.wait_ge(wv_loaded, 16)

            def keys(k):
                if k == 3:
                    pe.wait_ge(keys_loaded, 16 * 4)
                    for s in range(2):
                        for g in range(NHEAD // 2):
                            t = turn(bank[4 + s][:, g * P : (g + 1) * P], keys_in[:, s, g, :], ident[:])
                    t.then_inc(keys_turned, 1)
                if k == 5:
                    pe.wait_ge(keys_t_ready, 2)
                    for a in range(ND):
                        for s in range(2):
                            for h in range(NHEAD):
                                t = mm(bank[2 * a + s][:, h * NKEY : (h + 1) * NKEY],
                                       ffn_wq_in[:, 2 * h + s, a * P : (a + 1) * P],
                                       keys_t[:, s, h * NKEY : (h + 1) * NKEY], start=True, stop=True)
                    t.then_inc(keys_made, 1)

            def experts(it):
                if it == 1:
                    pe.wait_ge(up_lo_ready, NG)
                if it != 0:
                    return
                pe.wait_ge(keys_raw_ready, 2 * ND)
                pe.wait_ge(copied, copy_no(0, "sim3"))
                for g in range(NE * ND // 4):
                    a, q = g % ND, g // ND
                    pe.wait_ge(down_scaled, 4 * (q + 1))
                    after(pe, down_lo_ready, g - 7)
                    for i in range(4):
                        t = turn(bank[g % 8][:, i * P : (i + 1) * P], down_in[:, 4 * q + i, a * P : (a + 1) * P], ident[:])
                    t.then_inc(down_turned, 1)
                pe.wait_ge(down_lo_ready, NE * ND // 4)

            def product_with_up(it, k):
                n = (it - 2) * NPAIR + k
                j = (k - UP_LAG) % NPAIR
                after(pe, w_hi_ready, n - UP_LAG + 1)
                after_low_part(pe, it, k, UP_LAG)
                if j == 0:
                    after(pe, out_ready, it - 2)
                for t in range(NT):
                    for e in range(2):
                        cols = slice(t * P, (t + 1) * P)
                        mm(acc[t][:, 0 : 2 * D], w_hi[:, j % 2, e, cols],
                           up[:, 2 * j + e].rearrange("p q d -> p (q d)"),
                           start=(j == 0 and e == 0), stop=False)
                        u = mm(acc[t][:, 0:D], w_lo[:, j % 2, e, cols], up[:, 2 * j + e, 0, :],
                               start=False, stop=(j == NPAIR - 1 and e == 1))
                u.then_inc(up_done, 1)

            def body(it, stages):
                for k in range(SLOTS):
                    n = (it - 2) * NPAIR + k
                    if "dense" in stages:
                        if k == 0:
                            pe.wait_ge(z_lo_ready, it - 1)
                        after(pe, gelu_ready, n - 1)
                        for e in range(2):
                            j = 2 * k + e
                            terms = [(gp, zp, a) for gp, a in ((0, 0), (0, 1), (1, 0), (1, 1)) for zp in range(2 - gp)]
                            for i, (gp, zp, a) in enumerate(terms):
                                h = mm(h_ps[k % 2][:, e * NTOK : (e + 1) * NTOK], down_t[:, gp, a, j * P : (j + 1) * P],
                                       z16[:, (it + 1) % 3, zp, a, :], start=(i == 0), stop=(i == len(terms) - 1))
                        h.then_inc(h_filled, 1)
                    if lagged(stages, k, UP_LAG) and k >= S_AT[0]:
                        product_with_up(it, k)
                    if "pick" in stages:
                        b = it - 1
                        if k == TURN_AT:
                            pe.wait_ge(picks_ready, b + 1)
                            after(pe, s_stored, b * NG)
                            turned = s_ps[0][:].bitcast(F16)
                            for q in range(4):
                                t = turn(turned[:, q * P : (q + 1) * P], picks[:, q].rearrange("p t k -> p (t k)"),
                                         ident16[:])
                            t.then_inc(picks_turned, 1)
                        if k in S_AT:
                            g = S_AT.index(k)
                            pe.wait_ge(hot_ready, (b * NG + g + 1) * NT)
                            if g == 0:
                                pe.wait_ge(picks_t_ready, b + 1)
                            else:
                                pe.wait_ge(s_stored, b * NG + g)
                            for i in range(GT):
                                o = s_ps[i // HG][:].rearrange("p (j t) -> p j t", t=HG)
                                for part in range(2):
                                    m = mm(o[:, :, i % HG], hot_a[:, g % 2, :, i], hot_b[:, g % 2, part, :, i],
                                           start=(part == 0), stop=(part == 1))
                            m.then_inc(s_filled, 1)
                    if "front" in stages:
                        front(it, k)
                        if isinstance(it, int) and it == 0:
                            keys(k)
                    if lagged(stages, k, UP_LAG) and k < S_AT[0]:
                        product_with_up(it, k)
                    if "front" in stages and k == 7:
                        pe.wait_ge(z_ready, NT * (it + 1))
                        turn_tiles(f_ps[1], normed)

            def fill(m):
                m.then_inc(front_filled, 1)

            def turn_tiles(dst, src):
                for a in range(ND):
                    for t in range(NT):
                        m = turn(dst[:, a * NTOK + t * P : a * NTOK + (t + 1) * P], src[:, t, a * P : (a + 1) * P],
                                 ident[:])
                fill(m)

            def front(b, k):
                def from_(name):
                    pe.wait_ge(copied, copy_no(b, name))

                if k == 0:
                    pe.wait_ge(ctx_loaded, 16 * (b + 1))
                    after(pe, copied, copy_no(b - 1, "sim2") if not isinstance(b, int) or b > 0 else 0)
                    turn_tiles(f_ps[0], ctx_in)
                    pe.wait_ge(normed_ready, NT * (b + 1))
                    after(pe, copied, copy_no(b - 1, "sim3") if not isinstance(b, int) or b > 0 else 0)
                    turn_tiles(f_ps[1], normed)
                if k == 1:
                    from_("normed_t")
                    for c in range(ND):
                        for a in range(ND):
                            m = mm(f_ps[1][:, c * NTOK : (c + 1) * NTOK], wqk[:, a, c * P : (c + 1) * P],
                                   normed_t[:, a, :], start=(a == 0), stop=(a == ND - 1))
                    fill(m)
                if k == 2:
                    from_("q_t")
                    for t in range(NT):
                        for a in range(ND):
                            m = mm(f_ps[0][:, t * P : (2 * t + 1) * P], q_t[:, a, t * P : (t + 1) * P],
                                   ctx_t[:, a, 0 : (t + 1) * P], start=(a == 0), stop=(a == ND - 1))
                    fill(m)
                if k == 3:
                    for t in range(NT):
                        for a in range(ND):
                            m = mm(f_ps[1][:, t * D : (t + 1) * D], ctx_t[:, a, t * P : (t + 1) * P], wv[:, a, :],
                                   start=(a == 0), stop=(a == ND - 1))
                    fill(m)
                if k == 4:
                    pe.wait_ge(probs_ready, 2 * (b + 1))
                    for i in range(3):
                        m = turn(f_ps[0][:, i * P : (i + 1) * P], probs[:, i * P : (i + 1) * P], ident[:])
                    fill(m)
                if k == 5:
                    from_("probs_t")
                    for t, blocks in ((0, (0,)), (1, (1, 2))):
                        for i, c in enumerate(blocks):
                            m = mm(f_ps[1][:, t * D : (t + 1) * D], probs_t[:, c * P : (c + 1) * P], v[:, i, :],
                                   start=(i == 0), stop=(i == len(blocks) - 1))
                    fill(m)
                if 8 <= k < 12:
                    i = k - 8
                    t, c = i // 2, i % 2
                    if i == 0:
                        if isinstance(b, int) and b == 0:
                            pe.wait_ge(keys_q_ready, 1)
                        from_("z_hi")
                        pe.wait_ge(z_lo_ready, b + 1)
                    else:
                        from_(f"sim{i - 2}") if i >= 2 else None
                    terms = [(zp, kp, a) for a in range(ND) for zp, kp in ((0, 0), (0, 1), (1, 0))]
                    for j, (zp, kp, a) in enumerate(terms):
                        m = mm(f_ps[c][:, :], z16[:, b % 3, zp, a, t * P : (t + 1) * P],
                               keys_q[:, kp, a, c * BANK : (c + 1) * BANK], start=(j == 0), stop=(j == len(terms) - 1))
                    fill(m)

            passes(pe, body, experts)


_INS = ["x", "ctx_1024", "L0_xattn_w_q", "L0_xattn_w_k", "L0_xattn_w_v", "L0_ffn_w_q", "L0_ffn_keys",
        "L0_ffn_expert_down", "L0_ffn_expert_up", "L0_ffn_norm_w"]


def kernel(**inputs):
    import numpy as np
    import concourse.bacc as bacc
    from concourse.bass_utils import run_bass_kernel_spmd

    nc = bacc.Bacc("TRN2", target_bir_lowering=False, num_devices=1)
    arrays, args = {}, []
    for name in _INS:
        a = np.ascontiguousarray(inputs[name])
        arrays[f"in_{name}"] = a
        args.append(nc.dram_tensor(f"in_{name}", a.shape, mybir.dt.from_np(a.dtype), kind="ExternalInput").ap())
    shape = arrays["in_x"].shape
    args.append(nc.dram_tensor("out_dram", shape, mybir.dt.float32, kind="ExternalOutput").ap())
    cross_attention_and_expert_ffn(nc, *args)
    return run_bass_kernel_spmd(nc, [arrays], core_ids=[0]).results[0]["out_dram"]
```
